# Optimizing a Trainium2 kernel written in Bass

```python
import numpy as np
import jax
import jax.numpy as jnp

def _softmax(x, axis=-1):
    return jax.nn.softmax(x, axis=axis)

def _gelu(x):
    return jax.nn.gelu(x, approximate=True)

def _silu(x):
    return jax.nn.silu(x)

def _sigmoid(x):
    return jax.nn.sigmoid(x)

def _layernorm(x, axis=-1, eps=1e-05):
    m = jnp.mean(x, axis=axis, keepdims=True)
    v = jnp.var(x, axis=axis, keepdims=True)
    return (x - m) / jnp.sqrt(v + eps)

def _scatter_add(tgt, idx, src, axis=0):
    return tgt.at[idx].add(src)

def _segment_sum(src, seg, n):
    return jax.ops.segment_sum(src, seg, n)
kernel_name = 'mk_recurrent_d1_jaxref_r8_9c4b99'

def setup_inputs(seed: int=0):
    np.random.seed(seed)
    _w = jnp.asarray

    def _L0_attn_setup():
        import jax, jax.numpy as jnp
        import numpy as np
        N_STATE = 64
        SEQ_L = 512
        BATCH, HCH = (16, 64)
        DT_MIN, DT_MAX = (0.001, 0.1)

        def _make_DPLR_HiPPO(N):
            P = np.sqrt(1 + 2 * np.arange(N))
            A = P[:, None] * P[None, :]
            A = np.tril(A) - np.diag(np.arange(N))
            nhippo = -A
            p = 0.5 * np.sqrt(2 * np.arange(1, N + 1) + 1.0)
            q = 2 * p
            S = nhippo + p[:, None] * q[None, :]
            Lambda, V = np.linalg.eig(S)
            Vc = V.conj().T
            p_t = Vc @ p
            q_t = Vc @ q.conj()
            return (Lambda, p_t, q_t, Vc)

        def _ri(z):
            return np.stack([z.real, z.imag], axis=-1).astype(np.float32)

        def _cplx(x_ri):
            return x_ri[..., 0] + 1j * x_ri[..., 1]

        def _s4_kernel(Lambda, p, q, B, Ct, step, L):
            Omega = jnp.exp(-2j * jnp.pi * (jnp.arange(L) / L))
            g = 2.0 / step * ((1.0 - Omega) / (1.0 + Omega))
            c = 2.0 / (1.0 + Omega)
            denom = g[:, None] - Lambda[None, :]
            cauchy = lambda v: (v[None, :] / denom).sum(-1)
            k00 = cauchy(Ct.conj() * B)
            k01 = cauchy(Ct.conj() * p)
            k10 = cauchy(q.conj() * B)
            k11 = cauchy(q.conj() * p)
            at_roots = c * (k00 - k01 * (1.0 / (1.0 + k11)) * k10)
            return jnp.fft.ifft(at_roots, L).real
        key = jax.random.key(seed)
        k_u, k_ct, k_b, k_d, k_ls = jax.random.split(key, 5)
        Lambda, p, q, Vc = _make_DPLR_HiPPO(N_STATE)
        u = jax.random.normal(k_u, (BATCH, HCH, SEQ_L), dtype=jnp.float32)
        Ct_ri = jax.random.normal(k_ct, (1, N_STATE, 2), dtype=jnp.float32) / np.sqrt(N_STATE)
        Bp = jax.random.normal(k_b, (N_STATE, 1), dtype=jnp.float32) / np.sqrt(N_STATE)
        D = jax.random.uniform(k_d, (1,), dtype=jnp.float32)
        log_step = jax.random.uniform(k_ls, (1,), dtype=jnp.float32, minval=np.log(DT_MIN), maxval=np.log(DT_MAX))
        return {'u': u, 'Lambda_ri': jnp.asarray(_ri(Lambda)), 'p_ri': jnp.asarray(_ri(p)), 'q_ri': jnp.asarray(_ri(q)), 'Vc_ri': jnp.asarray(_ri(Vc)), 'Ct_ri': Ct_ri, 'Bp': Bp, 'D': D, 'log_step': log_step}
    _L0_attn_in = _L0_attn_setup()

    def _L0_ffn_setup():
        import jax, jax.numpy as jnp
        import numpy as np
        DIM = 512
        HID = 1376
        R = 16
        SCALING = 32.0 / 16.0

        def _lora_linear(x, w, a, b):
            base = jnp.einsum('bsd,od->bso', x, w)
            low = jnp.einsum('bsr,or->bso', jnp.einsum('bsd,rd->bsr', x, a), b)
            return base + low * SCALING
        key = jax.random.key(seed)
        ks = jax.random.split(key, 10)
        s_in = 1.0 / np.sqrt(DIM)
        s_hid = 1.0 / np.sqrt(HID)
        return {'x': jax.random.normal(ks[0], (4, 256, DIM), jnp.float32), 'w1': jax.random.normal(ks[1], (HID, DIM), jnp.float32) * s_in, 'w3': jax.random.normal(ks[2], (HID, DIM), jnp.float32) * s_in, 'w2': jax.random.normal(ks[3], (DIM, HID), jnp.float32) * s_hid, 'lora_A1': jax.random.normal(ks[4], (R, DIM), jnp.float32) * s_in, 'lora_B1': jax.random.normal(ks[5], (HID, R), jnp.float32) * 0.02, 'lora_A3': jax.random.normal(ks[6], (R, DIM), jnp.float32) * s_in, 'lora_B3': jax.random.normal(ks[7], (HID, R), jnp.float32) * 0.02, 'lora_A2': jax.random.normal(ks[8], (R, HID), jnp.float32) * s_hid, 'lora_B2': jax.random.normal(ks[9], (DIM, R), jnp.float32) * 0.02}
    _L0_ffn_in = _L0_ffn_setup()
    _d = {'L0_attn_u': _L0_attn_in['u'], 'L0_attn_Lambda_ri': _L0_attn_in['Lambda_ri'], 'L0_attn_p_ri': _L0_attn_in['p_ri'], 'L0_attn_q_ri': _L0_attn_in['q_ri'], 'L0_attn_Vc_ri': _L0_attn_in['Vc_ri'], 'L0_attn_Ct_ri': _L0_attn_in['Ct_ri'], 'L0_attn_Bp': _L0_attn_in['Bp'], 'L0_attn_D': _L0_attn_in['D'], 'L0_attn_log_step': _L0_attn_in['log_step'], 'L0_ffn_w1': _L0_ffn_in['w1'], 'L0_ffn_w3': _L0_ffn_in['w3'], 'L0_ffn_w2': _L0_ffn_in['w2'], 'L0_ffn_lora_A1': _L0_ffn_in['lora_A1'], 'L0_ffn_lora_B1': _L0_ffn_in['lora_B1'], 'L0_ffn_lora_A3': _L0_ffn_in['lora_A3'], 'L0_ffn_lora_B3': _L0_ffn_in['lora_B3'], 'L0_ffn_lora_A2': _L0_ffn_in['lora_A2'], 'L0_ffn_lora_B2': _L0_ffn_in['lora_B2']}
    _x0 = _d['L0_attn_u']
    _d['L0_attn_u'] = jax.random.normal(jax.random.fold_in(jax.random.key(seed), 1), (2, 1024, 512), dtype=_x0.dtype)
    del _x0
    return _d

def reference(L0_attn_u, L0_attn_Lambda_ri, L0_attn_p_ri, L0_attn_q_ri, L0_attn_Vc_ri, L0_attn_Ct_ri, L0_attn_Bp, L0_attn_D, L0_attn_log_step, L0_ffn_w1, L0_ffn_w3, L0_ffn_w2, L0_ffn_lora_A1, L0_ffn_lora_B1, L0_ffn_lora_A3, L0_ffn_lora_B3, L0_ffn_lora_A2, L0_ffn_lora_B2):

    def _L0_attn_ref(u, Lambda_ri, p_ri, q_ri, Vc_ri, Ct_ri, Bp, D, log_step):
        import jax, jax.numpy as jnp
        import numpy as np
        N_STATE = 64
        SEQ_L = 512
        BATCH, HCH = (16, 64)
        DT_MIN, DT_MAX = (0.001, 0.1)

        def _make_DPLR_HiPPO(N):
            P = np.sqrt(1 + 2 * np.arange(N))
            A = P[:, None] * P[None, :]
            A = np.tril(A) - np.diag(np.arange(N))
            nhippo = -A
            p = 0.5 * np.sqrt(2 * np.arange(1, N + 1) + 1.0)
            q = 2 * p
            S = nhippo + p[:, None] * q[None, :]
            Lambda, V = np.linalg.eig(S)
            Vc = V.conj().T
            p_t = Vc @ p
            q_t = Vc @ q.conj()
            return (Lambda, p_t, q_t, Vc)

        def _ri(z):
            return np.stack([z.real, z.imag], axis=-1).astype(np.float32)

        def _cplx(x_ri):
            return x_ri[..., 0] + 1j * x_ri[..., 1]

        def _s4_kernel(Lambda, p, q, B, Ct, step, L):
            Omega = jnp.exp(-2j * jnp.pi * (jnp.arange(L) / L))
            g = 2.0 / step * ((1.0 - Omega) / (1.0 + Omega))
            c = 2.0 / (1.0 + Omega)
            denom = g[:, None] - Lambda[None, :]
            cauchy = lambda v: (v[None, :] / denom).sum(-1)
            k00 = cauchy(Ct.conj() * B)
            k01 = cauchy(Ct.conj() * p)
            k10 = cauchy(q.conj() * B)
            k11 = cauchy(q.conj() * p)
            at_roots = c * (k00 - k01 * (1.0 / (1.0 + k11)) * k10)
            return jnp.fft.ifft(at_roots, L).real
        L = u.shape[-1]
        Lambda = _cplx(Lambda_ri)
        p = _cplx(p_ri)
        q = _cplx(q_ri)
        Vc = _cplx(Vc_ri)
        Ct = _cplx(Ct_ri).reshape(-1)
        B = (Vc @ Bp.astype(Vc.dtype)).reshape(-1)
        step = jnp.exp(log_step)[0]
        K = _s4_kernel(Lambda, p, q, B, Ct, step, L).astype(u.dtype)
        n = 2 * L
        y = jnp.fft.irfft(jnp.fft.rfft(u, n=n) * jnp.fft.rfft(K, n=n), n=n)[..., :L]
        return y + D[0] * u

    def _L0_ffn_ref(x, w1, w3, w2, lora_A1, lora_B1, lora_A3, lora_B3, lora_A2, lora_B2):
        import jax, jax.numpy as jnp
        import numpy as np
        DIM = 512
        HID = 1376
        R = 16
        SCALING = 32.0 / 16.0

        def _lora_linear(x, w, a, b):
            base = jnp.einsum('bsd,od->bso', x, w)
            low = jnp.einsum('bsr,or->bso', jnp.einsum('bsd,rd->bsr', x, a), b)
            return base + low * SCALING
        h1 = _lora_linear(x, w1, lora_A1, lora_B1)
        h3 = _lora_linear(x, w3, lora_A3, lora_B3)
        g = jax.nn.silu(h1) * h3
        return _lora_linear(g, w2, lora_A2, lora_B2)
    x = L0_attn_u
    xn = _layernorm(x, axis=-1)
    s = _L0_attn_ref(xn, L0_attn_Lambda_ri, L0_attn_p_ri, L0_attn_q_ri, L0_attn_Vc_ri, L0_attn_Ct_ri, L0_attn_Bp, L0_attn_D, L0_attn_log_step)
    g = _silu(_L0_ffn_ref(xn, L0_ffn_w1, L0_ffn_w3, L0_ffn_w2, L0_ffn_lora_A1, L0_ffn_lora_B1, L0_ffn_lora_A3, L0_ffn_lora_B3, L0_ffn_lora_A2, L0_ffn_lora_B2))
    x = x + s * g
    return x

_drawn_inputs = setup_inputs


def setup_inputs(seed=0):
    import zlib

    import numpy as np

    out = dict(_drawn_inputs(seed))
    spreads = {}
    factors = {'L0_attn_Lambda_ri': 8.0,
     'L0_attn_p_ri': 8.0,
     'L0_attn_q_ri': 8.0,
     'L0_attn_Vc_ri': 8.0,
     'L0_attn_Ct_ri': 8.0,
     'L0_attn_Bp': 8.0,
     'L0_ffn_lora_A1': 3.743,
     'L0_ffn_lora_B1': 3.766,
     'L0_ffn_lora_A3': 2.892,
     'L0_ffn_lora_B3': 2.887,
     'L0_ffn_lora_A2': 2.92,
     'L0_ffn_lora_B2': 2.964}
    for name, (base, spread) in spreads.items():
        noise = np.random.default_rng([zlib.crc32(name.encode()), seed]).standard_normal(out[name].shape)
        drawn = base * np.exp(spread * noise) if base else spread * noise
        out[name] = jnp.asarray(drawn.astype(out[name].dtype))
    for name, factor in factors.items():
        out[name] = (out[name] * factor).astype(out[name].dtype)
    return out
```

```python
from contextlib import ExitStack

import numpy as np
import concourse.bass as bass
from concourse import mybir

ALU = mybir.AluOpType
ACT = mybir.ActivationFunctionType
F32 = mybir.dt.float32
F32R = mybir.dt.float32r

P = 128
D = 512
HID = 1376
R = 16
LORA_SCALE = 2.0
ROWS = 2048
NS = 64
BLK = 512
NBLK = ROWS // BLK
RT = BLK // P
DC = D // P
HT = (HID + P - 1) // P
EPS = 1e-5
CL = 14


def hs(j):
    return min(P, HID - j * P)


A_COL = {1: 0, 3: D, 2: 2 * D + 2 * HID}
B_COL = {1: 2 * D, 3: 2 * D + HID, 2: 2 * D + 3 * HID}
LORA_COLS = 3 * D + 3 * HID

FOLD_FIRST = [(1, 0), (3, 0), (1, 1), (3, 1), (2, 0)]


def folds(place, j):
    if place == "gate":
        return [(1, j + 2)] if j + 2 < HT else []
    if place == "up":
        return [(3, j + 2)] if j + 2 < HT else []
    return [(2, t) for t in ([9, 10] if j == 8 else [j + 1] if j < 8 else [])]


FOLDS = FOLD_FIRST + [f for j in range(HT) for p in ("gate", "up", "down") for f in folds(p, j)]
FOLD_NO = {f: n for n, f in enumerate(FOLDS)}

TURN_AT_FIRST = {(9, "up"): 0, (9, "down"): 1, (10, "gate"): 2, (10, "up"): 3}
TURN_AT = {(3, "down"): 0, (4, "down"): 1, (5, "down"): 2, (6, "down"): 3}


def spare_uses():
    uses = [("fold", (1, 0)), ("fold", (3, 0)), ("turn", 0, 0), ("turn", 0, 1), ("turn", 0, 2), ("turn", 0, 3),
            ("B",), ("fold", (1, 1)), ("fold", (3, 1)), ("fold", (2, 0))]
    for j in range(HT):
        for place in ("gate", "up", "down"):
            uses += [("fold", f) for f in folds(place, j)]
            if (j, place) in TURN_AT_FIRST:
                uses.append(("turn", 1, TURN_AT_FIRST[j, place]))
            if (j, place) == (1, "down"):
                uses.append(("kappa",))
            if (j, place) == (3, "down"):
                uses.append(("krow",))
    if len(uses) % 2:
        uses.append(("none",))
    return uses + [("conv", 0, 0), ("conv", 0, 1)]


SPARE = {use: (n % 2, n // 2) for n, use in enumerate(spare_uses())}
SPARE_N = (SPARE["conv", 0, 0][1] + 1, SPARE["conv", 0, 1][1] + 1)
SPARE_SKIP = ("none",) in SPARE
if SPARE_SKIP:
    b_, n_ = SPARE[("none",)]
    SPARE = {u: (b, n - (b == b_ and n > n_)) for u, (b, n) in SPARE.items()}
    SPARE_N = (SPARE["conv", 0, 0][1] + 1, SPARE["conv", 0, 1][1] + 1)


def spare(b, use, first):
    if first:
        return SPARE[use]
    kind, _, r = use
    last = isinstance(b, int) and b == NBLK - 1
    later = 3 * (b - 1) + (r // 2 if kind == "turn" else 0 if last else 2)
    return r % 2, SPARE_N[r % 2] + later


def s4_constants():
    L = D
    lane = np.arange(L // 2)
    mirror = np.where(lane == 0, L // 2, L - lane)
    l = np.concatenate([lane, mirror])
    half = np.pi * l / L
    trig = np.concatenate([np.sin(half), np.cos(half)])[None, :].astype(np.float32)
    cosc = np.cos(half).reshape(4, P).T
    mask = np.ones((P, 2))
    mask[0, 0] = 0.0
    sign = np.where(np.arange(P) < NS, 1.0, -1.0)[:, None]
    powers = np.tile([-0.5, np.e, -1.0, -1.0, -1.0, -1.0, EPS], (P, 1))
    lanes = np.concatenate([cosc, mask, sign, powers, np.eye(P)], axis=1).astype(np.float32)
    t = np.arange(L) + 0.5
    lc, ls = lane, np.where(lane == 0, L // 2, lane)
    cos_rows = np.cos(2 * np.pi * ((lc[:, None] * t[None, :]) % L) / L) / L
    sin_rows = -np.sin(2 * np.pi * ((ls[:, None] * t[None, :]) % L) / L) / L
    dft = np.concatenate([cos_rows, sin_rows]).reshape(4, P, L).transpose(1, 0, 2).astype(np.float32)
    return trig, lanes, np.ascontiguousarray(dft)


def build(nc, x, xT, w1, w3, w2, lora, s4_lanes, s4_vc, s4_bp, s4_scalars, trig, lanes, dft, outT):
    ctx = ExitStack()
    with ctx:
        base = (nc.sbuf_base + 63) // 64 * 64

        def at(name, shape, off, dt=F32):
            return nc.alloc_sbuf_tensor_at(name, shape, dt, offset=base + off)

        top = [0]

        def put(name, shape, dt=F32):
            off = (top[0] + 31) // 32 * 32
            top[0] = off + int(np.prod(shape[1:])) * 4
            return at(name, shape, off, dt)

        w13 = put("w13", [P, 4 * DC * HID], F32R)
        w2f_off = top[0]
        w2f = put("w2f", [P, HT, 2, D], F32R)
        xt_off = top[0]
        xt = put("xt", [P, 2, 2, DC, BLK], F32R)
        lora_off = top[0]
        lr = put("lora_sb", [R, LORA_COLS])
        g = put("g", [P, BLK])
        ghl = put("ghl", [P, 2, BLK], F32R)
        xn = put("xn", [P, 4, D])
        tz = put("tz", [P, D])
        tzs = put("tzs", [P, 2, D], F32R)
        lane_c = put("lane_c", [P, CL + P])
        lane_d = put("lane_d", [P, 8])
        stats = put("stats", [P, 2, 6])
        moments = put("moments", [P, 4, 2])
        rstd = put("rstd", [P, 4])
        bp_sb = put("bp_sb", [NS, 1])
        scal = put("scal", [P, 2])
        small = put("small", [P, 8])
        bvec = put("bvec", [P, 2])
        vmat = put("vmat", [P, 8])
        vtmp = put("vtmp", [P, 16])
        kap = put("kap", [P, 4, 8])
        cplx = put("cplx", [P, 12, 4])
        coef = put("coef", [P, 4])
        assert base + top[0] <= nc.sbuf_usable_end
        raw = at("raw", [P, 6, BLK], xt_off + 2 * DC * BLK * 4)
        s4_tile = 5
        top[0] = w2f_off + s4_tile * 2 * D * 4
        trig_sb = put("trig_sb", [P, 2, D])
        den_re = put("den_re", [P, D])
        den_im = put("den_im", [P, D])
        mag = put("mag", [P, D])
        res = put("res", [P, D])
        dft_sb = put("dft_sb", [P, 4, D])
        vc_sb = put("vc_sb", [NS, 2 * P])
        krow = put("krow", [P, P + D])
        assert top[0] <= w2f_off + HT * 2 * D * 4
        xres = at("xres", [P, DC, BLK], lora_off)
        gate = at("gate", [P, 2, BLK], lora_off + DC * BLK * 4)

        k_dram = nc.dram_tensor("k_scratch", [P, P + D], F32, kind="Internal")

        def bank(name):
            return ctx.enter_context(nc.psum_tensor(name, [P, BLK], F32))

        h1, h3 = bank("h1"), bank("h3")
        sp = [bank("spare0"), bank("spare1")]
        f = [bank(f"f{i}") for i in range(DC)]
        conv = [sp[0], sp[1], h1, h3]
        OUT_ORDER = (2, 3, 0, 1)

        def sem(name):
            return ctx.enter_context(nc.semaphore(name))

        x_in = [sem(f"x_in{i}") for i in range(4)]
        raw_in = [sem(f"raw_in{i}") for i in range(6)]
        lora_in, const_in, s4_in, res_in, out_done = map(sem, ("lora_in", "const_in", "s4_in", "res_in", "out_done"))
        moments_ready, eps_added, rstd_ready, xn_ready, xt_turned = map(sem, ("moments_ready", "eps_added", "rstd_ready", "xn_ready", "xt_turned"))
        stats_done, stats_seen, xhi_done, xlo_done = map(sem, ("stats_done", "stats_seen", "xhi_done", "xlo_done"))
        spare_free = [sem("spare_free0"), sem("spare_free1")]
        fold_ready, fold_added, whi_done, wlo_done = map(sem, ("fold_ready", "fold_added", "whi_done", "wlo_done"))
        h1_ready, h3_ready, silu_done, g_done, ghi_done, glo_done, g_used = map(
            sem, ("h1_ready", "h3_ready", "silu_done", "g_done", "ghi_done", "glo_done", "g_used"))
        conv_ready, f_ready, gate_done, conv_used, res_done = map(
            sem, ("conv_ready", "f_ready", "gate_done", "conv_used", "res_done"))
        b_ready, b_copied, v_ready, kappa_ready, kappa_copied, coef_ready = map(
            sem, ("b_ready", "b_copied", "v_ready", "kappa_ready", "kappa_copied", "coef_ready"))
        mag_ready, inv_ready, res_ready, krow_ready, krow_copied, krow_done = map(
            sem, ("mag_ready", "inv_ready", "res_ready", "krow_ready", "krow_copied", "krow_done"))
        k_stored, tz_in, tz_hi, tz_lo, s4_step = map(sem, ("k_stored", "tz_in", "tz_hi", "tz_lo", "s4_step"))

        def w13_tile(kind, j, hl):
            n = DC * hs(j)
            s = 4 * DC * P * j + ((kind // 2) * 2 + hl) * n
            return w13[:, s:s + n].rearrange("p (c u) -> p c u", c=DC)

        def folded(kind, j, hl):
            if kind == 2:
                return w2f[0:hs(j), j, hl, :]
            n = DC * hs(j)
            s = 4 * DC * P * j + ((kind // 2) * 2 + hl) * n
            return w13[:, s:s + n]

        def raw_slot(kind, j):
            return (kind - 1) * 2 + j % 2

        def raw_tile(kind, j):
            s = raw_slot(kind, j)
            return raw[0:hs(j), s, :] if kind == 2 else raw[:, s, 0:DC * hs(j)]

        def fold_cols(kind, j):
            return D if kind == 2 else DC * hs(j)

        block = ctx.enter_context(nc.Block())

        @block.sync
        def _(sync):
            def load_rows(b, r, first):
                i = b * RT + r
                if not first:
                    sync.wait_ge(xt_turned, i - 3)
                sync.dma_start(xn[:, r, :], x[bass.ds(i * P, P), :]).then_inc(x_in[r], 16)

            def load_raw(kind, j):
                if j >= 2:
                    sync.wait_ge(wlo_done, FOLD_NO[kind, j - 2] + 1)
                if kind == 2:
                    src = w2[j * P:j * P + hs(j), :]
                else:
                    src = (w1 if kind == 1 else w3)[:, DC * P * j:DC * P * j + DC * hs(j)]
                sync.dma_start(raw_tile(kind, j), src).then_inc(raw_in[raw_slot(kind, j)], 16)

            def load_residual(b):
                sync.dma_start(xres[:, :, :], xT[:, :, bass.ds(b * BLK, BLK)]).then_inc(res_in, 16)

            def store(b):
                for n, c in enumerate(OUT_ORDER):
                    sync.wait_ge(res_done, b * DC + n + 1)
                    sync.dma_start(outT[c * P:(c + 1) * P, bass.ds(b * BLK, BLK)], xres[:, c, :]).then_inc(out_done, 16)

            def rest(b, last):
                if not last:
                    for r in range(RT):
                        load_rows(b + 1, r, False)
                sync.wait_ge(out_done, b * (DC * 16))
                load_residual(b)
                store(b)

            load_rows(0, 0, True)
            sync.dma_start(lr[:, :], lora).then_inc(lora_in, 16)
            load_rows(0, 1, True)
            load_raw(1, 0)
            load_rows(0, 2, True)
            load_raw(3, 0)
            load_rows(0, 3, True)
            for kind, j in FOLDS[2:14]:
                load_raw(kind, j)
            for r in range(RT):
                load_rows(1, r, False)
            for kind, j in FOLDS[14:]:
                load_raw(kind, j)
            sync.wait_ge(fold_ready, len(FOLDS))
            load_residual(0)
            store(0)
            with sync.Fori(1, NBLK - 1) as b:
                rest(b, False)
            rest(NBLK - 1, True)
            sync.wait_ge(out_done, NBLK * DC * 16)

        @block.scalar
        def _(act):
            def fold_hi(kind, j):
                act.wait_ge(fold_added, FOLD_NO[kind, j] + 1)
                nc.scalar.copy(folded(kind, j, 0), raw_tile(kind, j)).then_inc(whi_done, 1)

            def rows_hi(b, r, par, first):
                i = b * RT + r
                act.wait_ge(xt_turned, i + 1)
                if first and r == 0 and b == 1:
                    act.wait_ge(wlo_done, len(FOLDS))
                if not first:
                    act.wait_ge(conv_ready, (b - 1) * DC)
                bk, _ = spare(b - 1, ("turn", b, r), first)
                nc.scalar.copy(xt[:, par, 0, :, r * P:(r + 1) * P],
                               sp[bk][:, :].rearrange("p (c u) -> p c u", c=DC)).then_inc(xhi_done, 1)

            def hidden(b, j):
                t = b * HT + j
                act.wait_ge(h1_ready, t + 1)
                if not (isinstance(b, int) and t == 0):
                    act.wait_ge(glo_done, t)
                nc.scalar.activation(g[0:hs(j), :], h1[0:hs(j), :], ACT.Silu).then_inc(silu_done, 1)

            def hidden_hi(b, j):
                t = b * HT + j
                act.wait_ge(g_done, t + 1)
                if j > 0:
                    act.wait_ge(g_used, b * (HT - 1) + j)
                elif not isinstance(b, int) or b > 0:
                    act.wait_ge(f_ready, b * DC)
                nc.scalar.copy(ghl[0:hs(j), 0, :], g[0:hs(j), :]).then_inc(ghi_done, 1)

            def out_gate(b):
                for n, c in enumerate(OUT_ORDER):
                    e = b * DC + n
                    act.wait_ge(f_ready, e + 1)
                    if n >= 2:
                        act.wait_ge(res_done, e - 1)
                    elif not isinstance(b, int) or b > 0:
                        act.wait_ge(res_done, e - 1)
                    nc.scalar.activation(gate[:, n % 2, :], f[c][:, :], ACT.Silu).then_inc(gate_done, 1)

            def body(b, par_next, first, last):
                turn_at = TURN_AT_FIRST if first else TURN_AT
                for j in range(HT):
                    for place in ("gate", "up", "down"):
                        if place == "gate":
                            hidden(b, j)
                        if first:
                            for kind, t in folds(place, j):
                                fold_hi(kind, t)
                        if not last and (j, place) in turn_at:
                            rows_hi(b + 1, turn_at[j, place], par_next, first)
                        if place == "up":
                            hidden_hi(b, j)
                        if first and (j, place) == (1, "down"):
                            act.wait_ge(kappa_ready, 1)
                            nc.scalar.copy(kap[:, :, :], sp[SPARE[("kappa",)][0]][:, 0:32].rearrange("p (c k) -> p c k", c=4)) \
                                .then_inc(kappa_copied, 1)
                            act.wait_ge(kappa_copied, 1)
                            act.sem_inc(spare_free[SPARE[("kappa",)][0]], 1)
                        if first and (j, place) == (3, "down"):
                            act.wait_ge(krow_ready, 1)
                            nc.scalar.copy(krow[:, P:P + D], sp[SPARE[("krow",)][0]][:, :]).then_inc(krow_copied, 1)
                            act.wait_ge(krow_copied, 1)
                            act.sem_inc(spare_free[SPARE[("krow",)][0]], 1)
                        if first and (j, place) == (5, "up"):
                            act.wait_ge(tz_in, 16)
                            nc.scalar.copy(tzs[:, 0, :], tz[:, :]).then_inc(tz_hi, 1)
                out_gate(b)

            act.dma_start(lane_c[:, :], lanes).then_inc(const_in, 16)
            act.dma_start(lane_d[:, :], s4_lanes).then_inc(s4_in, 16)
            act.dma_start(scal[:, :], s4_scalars.to_broadcast([P, 2])).then_inc(s4_in, 16)
            act.dma_start(bp_sb[:, :], s4_bp).then_inc(s4_in, 16)
            act.dma_start(vc_sb[:, :], s4_vc).then_inc(s4_in, 16)
            act.dma_start(trig_sb[:, :, :].rearrange("p a l -> p (a l)"), trig.to_broadcast([P, 2 * D])).then_inc(s4_in, 16)
            act.dma_start(dft_sb[:, :, :], dft).then_inc(s4_in, 16)
            for r in range(RT):
                rows_hi(0, r, 0, True)
                if r == 0:
                    fold_hi(1, 0)
                if r == 1:
                    fold_hi(3, 0)
            act.wait_ge(b_ready, 1)
            nc.scalar.copy(bvec[:, :], sp[SPARE[("B",)][0]][:, 0:2]).then_inc(b_copied, 1)
            act.wait_ge(b_copied, 1)
            act.sem_inc(spare_free[SPARE[("B",)][0]], 1)
            for kind, j in FOLD_FIRST[2:]:
                fold_hi(kind, j)
            body(0, 1, True, False)
            with act.Fori(1, NBLK - 1) as b:
                body(b, (b + 1) % 2, False, False)
            body(NBLK - 1, None, False, True)

        @block.vector
        def _(dve):
            def fold_add(kind, j):
                n = FOLD_NO[kind, j]
                bk, use = SPARE["fold", (kind, j)]
                dve.wait_ge(raw_in[raw_slot(kind, j)], 16 * (j // 2 + 1))
                dve.wait_ge(fold_ready, n + 1)
                rt = raw_tile(kind, j)
                nc.vector.scalar_tensor_tensor(out=rt, in0=sp[bk][0:rt.shape[0], 0:fold_cols(kind, j)],
                                               scalar=LORA_SCALE, in1=rt, op0=ALU.mult, op1=ALU.add) \
                    .then_inc(fold_added, 1)
                dve.wait_ge(fold_added, n + 1)
                dve.sem_inc(spare_free[bk], 1)

            def fold_lo(kind, j):
                dve.wait_ge(whi_done, FOLD_NO[kind, j] + 1)
                nc.vector.tensor_tensor(folded(kind, j, 1), raw_tile(kind, j), folded(kind, j, 0).bitcast(F32),
                                        ALU.subtract).then_inc(wlo_done, 1)

            def rows_moments(b, r, round_):
                i = b * RT + r
                dve.wait_ge(x_in[r], 16 * (b + 1))
                nc.vector.bn_stats(stats[:, r % 2, :], xn[:, r, :]).then_inc(stats_done, 1)
                dve.wait_ge(stats_done, i + 1)
                dve.sem_inc(stats_seen, 1)
                nc.vector.bn_aggr(moments[:, r, :], stats[:, r % 2, :]).then_inc(moments_ready, 1)

            def rows_norm(b, r):
                i = b * RT + r
                dve.wait_ge(rstd_ready, i + 1)
                dve.wait_ge(moments_ready, i + 1)
                nc.vector.tensor_scalar(xn[:, r, :], xn[:, r, :], moments[:, r, 0:1], rstd[:, r:r + 1],
                                        ALU.subtract, ALU.mult).then_inc(xn_ready, 1)

            def rows_lo(b, r, par, first):
                i = b * RT + r
                bk, _ = spare(b - 1, ("turn", b, r), first)
                dve.wait_ge(xhi_done, i + 1)
                nc.vector.tensor_tensor(xt[:, par, 1, :, r * P:(r + 1) * P],
                                        sp[bk][:, :].rearrange("p (c u) -> p c u", c=DC),
                                        xt[:, par, 0, :, r * P:(r + 1) * P].bitcast(F32),
                                        ALU.subtract).then_inc(xlo_done, 1)
                dve.wait_ge(xlo_done, i + 1)
                dve.sem_inc(spare_free[bk], 1)

            def hidden_mul(b, j):
                t = b * HT + j
                dve.wait_ge(silu_done, t + 1)
                dve.wait_ge(h3_ready, t + 1)
                nc.vector.tensor_tensor(g[0:hs(j), :], g[0:hs(j), :], h3[0:hs(j), :], ALU.mult).then_inc(g_done, 1)

            def hidden_lo(b, j):
                t = b * HT + j
                dve.wait_ge(ghi_done, t + 1)
                nc.vector.tensor_tensor(ghl[0:hs(j), 1, :], g[0:hs(j), :], ghl[0:hs(j), 0, :].bitcast(F32),
                                        ALU.subtract).then_inc(glo_done, 1)

            def out_sum(b):
                for n, c in enumerate(OUT_ORDER):
                    e = b * DC + n
                    dve.wait_ge(gate_done, e + 1)
                    dve.wait_ge(conv_ready, (b + 1) * DC)
                    nc.vector.tensor_tensor(gate[:, n % 2, :], gate[:, n % 2, :], conv[c][:, :], ALU.mult) \
                        .then_inc(conv_used, 1)
                    dve.wait_ge(conv_used, e + 1)
                    if c < 2:
                        dve.sem_inc(spare_free[c], 1)
                    dve.wait_ge(res_in, 16 * (b + 1))
                    nc.vector.tensor_tensor(xres[:, c, :], xres[:, c, :], gate[:, n % 2, :], ALU.add) \
                        .then_inc(res_done, 1)

            def body(b, par_next, first, last):
                turn_at = TURN_AT_FIRST if first else TURN_AT
                for j in range(HT):
                    for place in ("gate", "up", "down"):
                        if place == "up":
                            hidden_mul(b, j)
                        if first:
                            for kind, t in folds(place, j):
                                fold_add(kind, t)
                                fold_lo(kind, t)
                        if place == "up":
                            if first and j == 0:
                                dve.wait_ge(mag_ready, 1)
                                nc.vector.reciprocal(mag[:, :], mag[:, :]).then_inc(inv_ready, 1)
                            hidden_lo(b, j)
                        if not last and (j, place) in turn_at:
                            rows_lo(b + 1, turn_at[j, place], par_next, first)
                        if not last and place == "down":
                            m = j - (5 if first else 0)
                            if 0 <= m < 4:
                                rows_moments(b + 1, m, None)
                            if 1 <= m < 5:
                                rows_norm(b + 1, m - 1)
                out_sum(b)

            rows_moments(0, 0, None)
            rows_moments(0, 1, None)
            rows_norm(0, 0)
            fold_add(1, 0)
            rows_moments(0, 2, None)
            rows_norm(0, 1)
            rows_lo(0, 0, 0, True)
            fold_lo(1, 0)
            fold_add(3, 0)
            rows_moments(0, 3, None)
            rows_norm(0, 2)
            rows_lo(0, 1, 0, True)
            fold_lo(3, 0)
            rows_norm(0, 3)
            rows_lo(0, 2, 0, True)
            rows_lo(0, 3, 0, True)
            for kind, j in FOLD_FIRST[2:]:
                fold_add(kind, j)
                fold_lo(kind, j)
            body(0, 1, True, False)
            with dve.Fori(1, NBLK - 1) as b:
                body(b, (b + 1) % 2, False, False)
            body(NBLK - 1, None, False, True)

        @block.tensor
        def _(pe):
            def take(b, use, first):
                bk, n = spare(b, use, first)
                if not isinstance(n, int) or n > 0:
                    pe.wait_ge(spare_free[bk], n)
                return sp[bk]

            def fold(kind, j):
                bankt = take(0, ("fold", (kind, j)), True)
                a, bc = A_COL[kind], B_COL[kind]
                if kind == 2:
                    mm = pe.matmul(bankt[0:hs(j), :], lr[:, a + j * P:a + j * P + hs(j)], lr[:, bc:bc + D],
                                   start=True, stop=True)
                else:
                    for c in range(DC):
                        mm = pe.matmul(bankt[:, c * hs(j):(c + 1) * hs(j)], lr[:, a + c * P:a + (c + 1) * P],
                                       lr[:, bc + j * P:bc + j * P + hs(j)], start=True, stop=True)
                mm.then_inc(fold_ready, 1)

            def turn_rows(b, r, first):
                i = b * RT + r
                bankt = take(b - 1, ("turn", b, r), first)
                pe.wait_ge(xn_ready, i + 1)
                for c in range(DC):
                    mm = pe.transpose(bankt[:, c * P:(c + 1) * P], xn[:, r, c * P:(c + 1) * P], lane_c[:, CL:CL + P])
                mm.then_inc(xt_turned, 1)

            def three(out, w, m, start, stop):
                pe.matmul(out, w[1], m[0], start=start, stop=False)
                pe.matmul(out, w[0], m[1], start=False, stop=False)
                return pe.matmul(out, w[0], m[0], start=False, stop=stop)

            def hidden(b, par, j, kind, out, ready):
                for c in range(DC):
                    mm = three(out[0:hs(j), :], [w13_tile(kind, j, hl)[:, c, :] for hl in (0, 1)],
                               [xt[:, par, hl, c, :] for hl in (0, 1)], c == 0, c == DC - 1)
                mm.then_inc(ready, 1)

            def down(b, j):
                t = b * HT + j
                pe.wait_ge(ghi_done, t + 1)
                pe.wait_ge(glo_done, t + 1)
                if j == 0 and (not isinstance(b, int) or b > 0):
                    pe.wait_ge(gate_done, b * DC)
                for n, c in enumerate(OUT_ORDER):
                    mm = three(f[c][:, :], [w2f[0:hs(j), j, hl, c * P:(c + 1) * P] for hl in (0, 1)],
                               [ghl[0:hs(j), hl, :] for hl in (0, 1)], j == 0, j == HT - 1)
                    if j == HT - 1:
                        mm.then_inc(f_ready, 1)
                    elif n == DC - 1:
                        mm.then_inc(g_used, 1)

            def convolve(b, par, c_out, first):
                t = b * HT + HT
                if c_out < 2:
                    out = take(b, ("conv", b, c_out), first)
                else:
                    pe.wait_ge((silu_done, g_done)[c_out - 2], t)
                    out = conv[c_out]
                for c in range(c_out + 1):
                    k = (c_out - c) * P
                    mm = three(out[:, :], [tzs[:, hl, k:k + P] for hl in (0, 1)],
                               [xt[:, par, hl, c, :] for hl in (0, 1)], c == 0, c == c_out)
                mm.then_inc(conv_ready, 1)

            def extras(b, j, place, first, last):
                if first:
                    for kind, t in folds(place, j):
                        fold(kind, t)
                turn_at = TURN_AT_FIRST if first else TURN_AT
                if not last and (j, place) in turn_at:
                    turn_rows(b + 1, turn_at[j, place], first)
                if first and (j, place) == (1, "down"):
                    bankt = take(0, ("kappa",), True)
                    pe.wait_ge(res_ready, 2)
                    pe.wait_ge(v_ready, 1)
                    for c in range(4):
                        mm = pe.matmul(bankt[:, 8 * c:8 * c + 8], res[:, c * P:(c + 1) * P], vmat[:, :], start=True, stop=True)
                    mm.then_inc(kappa_ready, 1)
                if first and (j, place) == (3, "down"):
                    bankt = take(0, ("krow",), True)
                    pe.wait_ge(coef_ready, 2)
                    for c in range(4):
                        mm = pe.matmul(bankt[:, :], coef[:, c:c + 1].to_broadcast([P, P]), dft_sb[:, c, :], start=(c == 0), stop=(c == 3))
                    mm.then_inc(krow_ready, 1)

            def body(b, par, first, last):
                pe.wait_ge(xlo_done, (b + 1) * RT)
                for j in range(HT):
                    t = b * HT + j
                    if first:
                        pe.wait_ge(wlo_done, FOLD_NO[1, j] + 1)
                    if j > 0:
                        pe.wait_ge(silu_done, t)
                    elif not first:
                        pe.wait_ge(conv_used, (b - 1) * DC + 1)
                    hidden(b, par, j, 1, h1, h1_ready)
                    extras(b, j, "gate", first, last)
                    if first:
                        pe.wait_ge(wlo_done, FOLD_NO[3, j] + 1)
                    if j > 0:
                        pe.wait_ge(g_done, t)
                    elif not first:
                        pe.wait_ge(conv_used, (b - 1) * DC + 2)
                    hidden(b, par, j, 3, h3, h3_ready)
                    extras(b, j, "up", first, last)
                    if j > 0:
                        if first:
                            pe.wait_ge(wlo_done, FOLD_NO[2, j - 1] + 1)
                        down(b, j - 1)
                    extras(b, j, "down", first, last)
                if first:
                    pe.wait_ge(tz_lo, 1)
                for c in range(DC):
                    convolve(b, par, c, first)
                if first:
                    pe.wait_ge(wlo_done, FOLD_NO[2, HT - 1] + 1)
                down(b, HT - 1)

            pe.wait_ge(lora_in, 16)
            fold(1, 0)
            fold(3, 0)
            pe.wait_ge(const_in, 16)
            for r in range(RT):
                turn_rows(0, r, True)
            bankt = take(0, ("B",), True)
            pe.wait_ge(s4_in, 16 * 6)
            for ri in range(2):
                mm = pe.matmul(bankt[:, ri:ri + 1], vc_sb[:, ri * P:(ri + 1) * P], bp_sb[:, :], start=True, stop=True)
            mm.then_inc(b_ready, 1)
            for kind, j in FOLD_FIRST[2:]:
                fold(kind, j)
            body(0, 0, True, False)
            with pe.Fori(1, NBLK - 1) as b:
                body(b, b % 2, False, False)
            body(NBLK - 1, (NBLK - 1) % 2, False, True)

        @block.gpsimd
        def _(pool):
            steps = [0]

            def then(ins):
                steps[0] += 1
                ins.then_inc(s4_step, 1)
                pool.wait_ge(s4_step, steps[0])

            def ts(out, a, s1, s2, op0, op1=None):
                if op1 is None:
                    return nc.gpsimd.tensor_scalar(out, a, s1, None, op0)
                return nc.gpsimd.tensor_scalar(out, a, s1, s2, op0, op1)

            def tt(out, a, c, op):
                return nc.gpsimd.tensor_tensor(out, a, c, op)

            def rows_rstd(b, r):
                pool.wait_ge(moments_ready, b * RT + r + 1)
                tt(rstd[:, r:r + 1], moments[:, r, 1:2], lane_c[:, 13:14], ALU.add).then_inc(eps_added, 1)
                pool.wait_ge(eps_added, b * RT + r + 1)
                tt(rstd[:, r:r + 1], rstd[:, r:r + 1], lane_c[:, 7:8], ALU.pow).then_inc(rstd_ready, 1)

            pool.wait_ge(const_in, 16)
            for r in range(RT):
                rows_rstd(0, r)
            S, C = trig_sb[:, 0, :], trig_sb[:, 1, :]
            pool.wait_ge(s4_in, 16 * 6)
            then(ts(small[:, 1:2], scal[:, 1:2], -1.0, None, ALU.mult))
            then(tt(small[:, 2:3], lane_c[:, 8:9], small[:, 1:2], ALU.pow))
            then(ts(small[:, 2:3], small[:, 2:3], 2.0, None, ALU.mult))
            then(ts(small[:, 3:5], lane_d[:, 0:2], -1.0, None, ALU.mult))
            then(ts(den_re[:, :], C, small[:, 3:4], None, ALU.mult))
            then(ts(den_im[:, :], C, small[:, 4:5], None, ALU.mult))
            then(ts(res[:, :], S, small[:, 2:3], None, ALU.mult))
            then(tt(den_im[:, :], den_im[:, :], res[:, :], ALU.add))
            then(tt(mag[:, :], den_re[:, :], den_re[:, :], ALU.mult))
            then(tt(res[:, :], den_im[:, :], den_im[:, :], ALU.mult))
            tt(mag[:, :], mag[:, :], res[:, :], ALU.add).then_inc(mag_ready, 1)
            then(ts(vtmp[:, 0:1], lane_d[:, 3:4], lane_c[:, 6:7], None, ALU.mult))
            then(ts(vtmp[:, 1:2], lane_d[:, 5:6], lane_c[:, 6:7], None, ALU.mult))
            pool.wait_ge(b_copied, 1)
            v = vmat[:, :].rearrange("p (k r) -> p k r", r=2)
            for ui, (ua, ub) in enumerate([(lane_d[:, 4:5], vtmp[:, 1:2]), (lane_d[:, 2:3], vtmp[:, 0:1])]):
                for wi, (wre, wim) in enumerate([(bvec[:, 0:1], bvec[:, 1:2]), (lane_d[:, 6:7], lane_d[:, 7:8])]):
                    k = 2 * ui + wi
                    then(tt(vtmp[:, 4:5], ua, wre, ALU.mult))
                    then(tt(vtmp[:, 5:6], ub, wim, ALU.mult))
                    then(tt(v[:, k, 0:1], vtmp[:, 4:5], vtmp[:, 5:6], ALU.add))
                    then(tt(vtmp[:, 6:7], ua, wim, ALU.mult))
                    then(tt(vtmp[:, 7:8], ub, wre, ALU.mult))
                    ins = tt(v[:, k, 1:2], vtmp[:, 6:7], vtmp[:, 7:8], ALU.subtract)
                    if k == 3:
                        ins.then_inc(v_ready, 1)
                        pool.wait_ge(v_ready, 1)
                    else:
                        then(ins)
            pool.wait_ge(inv_ready, 1)
            then(ts(den_im[NS:P, :], den_im[NS:P, :], -1.0, None, ALU.mult))
            tt(res[0:NS, :], den_re[0:NS, :], mag[0:NS, :], ALU.mult).then_inc(res_ready, 1)
            pool.wait_ge(res_ready, 1)
            tt(res[NS:P, :], den_im[NS:P, :], mag[NS:P, :], ALU.mult).then_inc(res_ready, 1)
            pool.wait_ge(res_ready, 2)
            pool.wait_ge(kappa_copied, 1)
            k00, k01, k10, k11 = [(kap[:, :, 2 * k], kap[:, :, 2 * k + 1]) for k in range(4)]
            cosl = lane_c[:, 0:4]
            q = [cplx[:, i, :] for i in range(12)]

            def cmul(re, im, a, c, t0, t1):
                then(tt(t0, a[0], c[0], ALU.mult))
                then(tt(t1, a[1], c[1], ALU.mult))
                then(tt(re, t0, t1, ALU.subtract))
                then(tt(t0, a[0], c[1], ALU.mult))
                then(tt(t1, a[1], c[0], ALU.mult))
                then(tt(im, t0, t1, ALU.add))

            cmul(q[2], q[3], k01, k10, q[0], q[1])
            then(tt(q[2], q[2], cosl, ALU.mult))
            then(tt(q[3], q[3], cosl, ALU.mult))
            then(tt(q[4], k11[0], cosl, ALU.mult))
            then(ts(q[4], q[4], 1.0, None, ALU.add))
            then(tt(q[5], k11[1], cosl, ALU.mult))
            then(tt(q[6], q[4], q[4], ALU.mult))
            then(tt(q[7], q[5], q[5], ALU.mult))
            then(tt(q[6], q[6], q[7], ALU.add))
            then(tt(q[6], q[6], lane_c[:, 9:13], ALU.pow))
            then(tt(q[4], q[4], q[6], ALU.mult))
            then(tt(q[5], q[5], q[6], ALU.mult))
            then(ts(q[5], q[5], -1.0, None, ALU.mult))
            cmul(q[8], q[9], (q[2], q[3]), (q[4], q[5]), q[0], q[1])
            then(tt(q[8], k00[0], q[8], ALU.subtract))
            then(tt(q[9], k00[1], q[9], ALU.subtract))
            m = lane_c[:, 4:6]
            then(tt(q[0][:, 0:2], q[8][:, 2:4], m, ALU.mult))
            then(tt(q[1][:, 0:2], q[9][:, 0:2], m, ALU.mult))
            tt(coef[:, 0:2], q[8][:, 0:2], q[0][:, 0:2], ALU.subtract).then_inc(coef_ready, 1)
            tt(coef[:, 2:4], q[1][:, 0:2], q[9][:, 2:4], ALU.add).then_inc(coef_ready, 1)
            then(nc.gpsimd.memset(krow[:, 0:P], 0.0))
            pool.wait_ge(krow_copied, 1)
            tt(krow[:, P:P + 1], krow[:, P:P + 1], scal[:, 0:1], ALU.add).then_inc(krow_done, 1)
            pool.wait_ge(krow_done, 1)
            pool.dma_start(k_dram[:, :], krow[:, :]).then_inc(k_stored, 16)
            pool.wait_ge(k_stored, 16)
            shifted = bass.AP(tensor=k_dram, offset=P, ap=[[P + D - 1, P], [1, D]])
            pool.dma_start(tz[:, :], shifted).then_inc(tz_in, 16)
            pool.wait_ge(tz_hi, 1)
            tt(tzs[:, 1, :], tz[:, :], tzs[:, 0, :].bitcast(F32), ALU.subtract).then_inc(tz_lo, 1)

            for r in range(RT):
                rows_rstd(1, r)
            with pool.Fori(1, NBLK - 1) as b:
                for r in range(RT):
                    rows_rstd(b + 1, r)


def kernel(L0_attn_u, L0_attn_Lambda_ri, L0_attn_p_ri, L0_attn_q_ri, L0_attn_Vc_ri, L0_attn_Ct_ri, L0_attn_Bp,
           L0_attn_D, L0_attn_log_step, L0_ffn_w1, L0_ffn_w3, L0_ffn_w2, L0_ffn_lora_A1, L0_ffn_lora_B1,
           L0_ffn_lora_A3, L0_ffn_lora_B3, L0_ffn_lora_A2, L0_ffn_lora_B2):
    import numpy as _np
    import concourse.bacc as _bacc
    from concourse import mybir as _mybir
    from concourse.bass_utils import run_bass_kernel_spmd as _run

    c = _np.ascontiguousarray

    def turned_tiles(w):
        wt = _np.asarray(w).T.reshape(DC, P, HID)
        return _np.concatenate([wt[:, :, j * P:j * P + hs(j)].transpose(1, 0, 2).reshape(P, -1) for j in range(HT)], axis=1)

    x = _np.asarray(L0_attn_u).reshape(ROWS, D)
    lam, p, q = (_np.asarray(a) for a in (L0_attn_Lambda_ri, L0_attn_p_ri, L0_attn_q_ri))
    ct, vc = _np.asarray(L0_attn_Ct_ri).reshape(NS, 2), _np.asarray(L0_attn_Vc_ri)
    twice = lambda a: _np.concatenate([a, a])
    lanes_d = _np.stack([twice(lam[:, 0]), twice(lam[:, 1]),
                         _np.concatenate([q[:, 0], q[:, 1]]), _np.concatenate([q[:, 1], q[:, 0]]),
                         _np.concatenate([ct[:, 0], ct[:, 1]]), _np.concatenate([ct[:, 1], ct[:, 0]]),
                         twice(p[:, 0]), twice(p[:, 1])], axis=1)
    vct = vc.transpose(1, 2, 0)
    vct = _np.concatenate([vct[:, 0], vct[:, 0], vct[:, 1], vct[:, 1]], axis=1)
    a1, b1, a3, b3, a2, b2 = (_np.asarray(a) for a in (L0_ffn_lora_A1, L0_ffn_lora_B1, L0_ffn_lora_A3,
                                                      L0_ffn_lora_B3, L0_ffn_lora_A2, L0_ffn_lora_B2))
    lora = _np.concatenate([a1, a3, b1.T, b3.T, a2, b2.T], axis=1)
    trig, lanes, dft = s4_constants()
    arrays = {
        "x": c(x), "xT": c(x.T.reshape(DC, P, ROWS).transpose(1, 0, 2)),
        "w1": c(turned_tiles(L0_ffn_w1)), "w3": c(turned_tiles(L0_ffn_w3)), "w2": c(_np.asarray(L0_ffn_w2).T),
        "lora": c(lora), "s4_lanes": c(lanes_d), "s4_vc": c(vct), "s4_bp": c(_np.asarray(L0_attn_Bp)),
        "s4_scalars": c(_np.stack([_np.asarray(L0_attn_D), _np.asarray(L0_attn_log_step)], axis=1)),
        "trig": trig, "lanes": lanes, "dft": dft,
    }
    nc = _bacc.Bacc("TRN2", target_bir_lowering=False, num_devices=1)
    args = [nc.dram_tensor(f"{k}_dram", a.shape, _mybir.dt.from_np(a.dtype), kind="ExternalInput").ap()
            for k, a in arrays.items()]
    args.append(nc.dram_tensor("outT_dram", (D, ROWS), F32, kind="ExternalOutput").ap())
    build(nc, *args)
    r = _run(nc, [{f"{k}_dram": a for k, a in arrays.items()}], core_ids=[0])
    return r.results[0]["outT_dram"].T.reshape(2, 1024, D)
```

```python
from contextlib import ExitStack

import numpy as np
import concourse.bass as bass
from concourse import mybir

ALU = mybir.AluOpType
ACT = mybir.ActivationFunctionType
F32 = mybir.dt.float32
F32R = mybir.dt.float32r

P = 128
D = 512
HID = 1376
R = 16
LORA_SCALE = 2.0
ROWS = 2048
NS = 64
BLK = 512
NBLK = ROWS // BLK
RT = BLK // P
DC = D // P
HT = (HID + P - 1) // P
EPS = 1e-5
CL = 16


def hs(j):
    return min(P, HID - j * P)


ST_COLS = 2 * D + HID
MV_COLS = 2 * HID + D
LORA_COLS = ST_COLS + MV_COLS
A_COL = {1: 0, 3: D, 2: 2 * D}
B_COL = {1: ST_COLS, 3: ST_COLS + HID, 2: ST_COLS + 2 * HID}
FIRST_COLS = {1: 2 * D, 3: 2 * D + 2 * P, 2: 2 * D + 5 * P}
LORA_FIRST = 3 * D + 5 * P
LANES_ST, LANES_MV = ST_COLS * R // P, MV_COLS * R // P
STACK = ((1, 0), (0, 1), (0, 0))
PLAIN = {1: 1, 3: 1, 2: 0}
A_FIRST = {1: 0, 3: D, 2: 2 * D + 4 * P}

FOLD_FIRST = [(1, 0), (3, 0), (1, 1), (3, 1), (2, 0)]


def folds(place, j):
    if j == 0 or j == HT - 1:
        return []
    if place == "down":
        return [(2, j)] if j < HT - 2 else [(2, HT - 2), (2, HT - 1)]
    return [(1 if place == "gate" else 3, j + 1)]


FOLDS = FOLD_FIRST + [f for j in range(HT) for p in ("gate", "up", "down") for f in folds(p, j)]
FOLD_NO = {f: n for n, f in enumerate(FOLDS)}
POOL_LO = [(3, 0), (3, 1)]
DVE_LO = [f for f in FOLDS if f not in POOL_LO]

TURN_AT_FIRST = {(10, "gate"): (0,), (10, "up"): (1,), (10, "down"): (2,), "out": (3,)}
TURN_AT = {(4, "down"): (0,), (5, "down"): (1,), (6, "down"): (2,), (7, "down"): (3,)}


RECIPROCAL_AT = [(2, "up"), (3, "gate")]

KAPPA_AT, KROW_AT = (4, "up"), (6, "up")
TOEPLITZ_AT = (8, "up")


def spare_uses():
    uses = [("fold", (1, 0)), ("fold", (3, 0)), ("fold", (1, 1)), ("fold", (3, 1)), ("fold", (2, 0)), ("B",)]
    for j in range(HT):
        for place in ("gate", "up", "down"):
            uses += [("fold", f) for f in folds(place, j)]
            uses += [("turn", 1, r) for r in TURN_AT_FIRST.get((j, place), ())]
            if (j, place) == KAPPA_AT:
                uses.append(("kappa",))
            if (j, place) == KROW_AT:
                uses.append(("krow",))
    uses += [("turn", 1, r) for r in TURN_AT_FIRST["out"]]
    if len(uses) % 2:
        uses.append(("none",))
    return uses + [("conv", 0, 0), ("conv", 0, 1)]


SPARE = {use: (n % 2, n // 2) for n, use in enumerate(spare_uses())}
SPARE_N = (SPARE["conv", 0, 0][1] + 1, SPARE["conv", 0, 1][1] + 1)
SPARE_SKIP = ("none",) in SPARE
if SPARE_SKIP:
    b_, n_ = SPARE[("none",)]
    SPARE = {u: (b, n - (b == b_ and n > n_)) for u, (b, n) in SPARE.items()}
    SPARE_N = (SPARE["conv", 0, 0][1] + 1, SPARE["conv", 0, 1][1] + 1)


def spare(b, use, first):
    if first:
        return SPARE[use]
    kind, _, r = use
    last = isinstance(b, int) and b == NBLK - 1
    later = 3 * (b - 1) + (r // 2 if kind == "turn" else 0 if last else 2)
    return r % 2, SPARE_N[r % 2] + later


def s4_constants():
    L = D
    lane = np.arange(L // 2)
    mirror = np.where(lane == 0, L // 2, L - lane)
    l = np.concatenate([lane, mirror])
    half = np.pi * l / L
    trig = np.concatenate([np.sin(half), np.cos(half)])[None, :].astype(np.float32)
    cosc = np.cos(half).reshape(4, P).T
    mask = np.ones((P, 2))
    mask[0, 0] = 0.0
    sign = np.where(np.arange(P) < NS, 1.0, -1.0)[:, None]
    powers = np.tile([-0.5, -0.5, np.e, -1.0, -1.0, -1.0, -1.0, EPS, EPS], (P, 1))
    lanes = np.concatenate([cosc, mask, sign, powers, np.eye(P)], axis=1).astype(np.float32)
    t = np.arange(L // 2) + 0.5
    lc, ls = lane, np.where(lane == 0, L // 2, lane)
    cos_rows = np.cos(2 * np.pi * ((lc[:, None] * t[None, :]) % L) / L) / L
    sin_rows = -np.sin(2 * np.pi * ((ls[:, None] * t[None, :]) % L) / L) / L
    dft = np.concatenate([cos_rows, sin_rows]).reshape(4, P, L // 2).transpose(1, 0, 2).astype(np.float32)
    return trig, lanes, np.ascontiguousarray(dft)


def build(nc, x, xT, w1, w3, w2, lora, lora_st, lora_mv, s4_lanes, s4_vc, s4_bp, s4_scalars, trig, lanes, dft, outT):
    ctx = ExitStack()
    with ctx:
        base = (nc.sbuf_base + 63) // 64 * 64

        def at(name, shape, off, dt=F32):
            return nc.alloc_sbuf_tensor_at(name, shape, dt, offset=base + off)

        top = [0]

        def put(name, shape, dt=F32):
            off = (top[0] + 31) // 32 * 32
            top[0] = off + int(np.prod(shape[1:])) * 4
            return at(name, shape, off, dt)

        w13 = put("w13", [P, 4 * DC * HID], F32R)
        w2f_off = top[0]
        w2f = put("w2f", [P, HT, 2, D], F32R)
        xt_off = top[0]
        xt = put("xt", [P, 2, 2, DC, BLK], F32R)
        lora_off = top[0]
        lst = put("lora_stack", [len(STACK) * R, LORA_COLS], F32R)
        g = put("g", [P, BLK])
        ghl = put("ghl", [P, 2, BLK], F32R)
        xn = put("xn", [P, 4, D])
        tz = put("tz", [P, D])
        tzs = put("tzs", [P, 2, D], F32R)
        lane_c = put("lane_c", [P, CL + P])
        lane_d = put("lane_d", [P, 8])
        stats = put("stats", [P, 2, 6])
        moments = put("moments", [P, 4, 2])
        rstd = put("rstd", [P, 4])
        shift = put("shift", [P, 4])
        bp_sb = put("bp_sb", [NS, 1])
        scal = put("scal", [P, 2])
        small = put("small", [P, 8])
        bvec = put("bvec", [P, 2])
        vmat = put("vmat", [P, 8])
        vtmp = put("vtmp", [P, 16])
        kap = put("kap", [P, 4, 8])
        cplx = put("cplx", [P, 12, 4])
        coef = put("coef", [P, 4])
        assert base + top[0] <= nc.sbuf_usable_end
        raw = at("raw", [P, 6, BLK], xt_off + 2 * DC * BLK * 4)
        lr = at("lora_first", [R, LORA_FIRST], 7 * 4 * DC * P * 4)
        spread = at("lora_spread", [P, LANES_ST + LANES_MV], 4 * 4 * DC * P * 4)
        spread_hl = at("lora_spread_split", [P, 2, LANES_ST + LANES_MV], 5 * 4 * DC * P * 4, F32R)
        s4_tile = 5
        top[0] = w2f_off + s4_tile * 2 * D * 4
        trig_sb = put("trig_sb", [P, 2, D])
        den_re = put("den_re", [P, D])
        den_im = put("den_im", [P, D])
        mag = put("mag", [P, D])
        res = put("res", [P, D])
        dft_sb = put("dft_sb", [P, 4, D // 2])
        even_odd = put("even_odd", [P, 2, D // 2])
        vc_sb = put("vc_sb", [NS, 2 * P])
        krow = put("krow", [P, P + D])
        assert top[0] <= w2f_off + HT * 2 * D * 4
        xres = at("xres", [P, DC, BLK], lora_off)
        gate = at("gate", [P, 2, BLK], lora_off + DC * BLK * 4)

        k_dram = nc.dram_tensor("k_scratch", [P, P + D], F32, kind="Internal")

        def bank(name):
            return ctx.enter_context(nc.psum_tensor(name, [P, BLK], F32))

        h1, h3 = bank("h1"), bank("h3")
        sp = [bank("spare0"), bank("spare1")]
        f = [bank(f"f{i}") for i in range(DC)]
        conv = [sp[0], sp[1], h3, h1]
        OUT_ORDER = (3, 2, 1, 0)

        def sem(name):
            return ctx.enter_context(nc.semaphore(name))

        x_in = [sem(f"x_in{i}") for i in range(4)]
        raw_in = [sem(f"raw_in{i}") for i in range(6)]
        lora_in, wlo_pool, bvec_in, dft_in, spread_in, spread_hi, spread_lo, stack_in, const_in, s4_in, res_in, out_done = map(sem, ("lora_in", "wlo_pool", "bvec_in", "dft_in", "spread_in", "spread_hi", "spread_lo", "stack_in", "const_in", "s4_in", "res_in", "out_done"))
        moments_ready, eps_added, rstd_ready, shift_step, shift_ready, xn_ready, xt_turned = map(sem, ("moments_ready", "eps_added", "rstd_ready", "shift_step", "shift_ready", "xn_ready", "xt_turned"))
        stats_done, stats_seen, xhi_done, xlo_done = map(sem, ("stats_done", "stats_seen", "xhi_done", "xlo_done"))
        spare_free = [sem("spare_free0"), sem("spare_free1")]
        fold_ready, fold_added, whi_done, wlo_done = map(sem, ("fold_ready", "fold_added", "whi_done", "wlo_done"))
        h1_ready, h3_ready, silu_done, g_done, ghi_done, glo_done, g_used, g_cleared = map(
            sem, ("h1_ready", "h3_ready", "silu_done", "g_done", "ghi_done", "glo_done", "g_used", "g_cleared"))
        conv_ready, f_ready, gate_done, conv_used, res_done = map(
            sem, ("conv_ready", "f_ready", "gate_done", "conv_used", "res_done"))
        b_ready, b_copied, v_ready, kappa_ready, kappa_copied, coef_ready = map(
            sem, ("b_ready", "b_copied", "v_ready", "kappa_ready", "kappa_copied", "coef_ready"))
        mag_ready, inv_ready, res_ready, krow_ready, krow_copied, krow_done = map(
            sem, ("mag_ready", "inv_ready", "res_ready", "krow_ready", "krow_copied", "krow_done"))
        k_stored, tz_in, tz_hi, tz_lo, s4_step = map(sem, ("k_stored", "tz_in", "tz_hi", "tz_lo", "s4_step"))

        def w13_tile(kind, j, hl):
            n = DC * hs(j)
            s = 4 * DC * P * j + ((kind // 2) * 2 + hl) * n
            return w13[:, s:s + n].rearrange("p (c u) -> p c u", c=DC)

        def folded(kind, j, hl):
            if kind == 2:
                return w2f[0:hs(j), j, hl, :]
            n = DC * hs(j)
            s = 4 * DC * P * j + ((kind // 2) * 2 + hl) * n
            return w13[:, s:s + n]

        def raw_slot(kind, j):
            return (kind - 1) * 2 + j % 2

        def raw_tile(kind, j):
            s = raw_slot(kind, j)
            return raw[0:hs(j), s, :] if kind == 2 else raw[:, s, 0:DC * hs(j)]

        def fold_cols(kind, j):
            return D if kind == 2 else DC * hs(j)

        def wait_split(eng, kind, j):
            if (kind, j) in POOL_LO:
                eng.wait_ge(wlo_pool, POOL_LO.index((kind, j)) + 1)
            else:
                eng.wait_ge(wlo_done, DVE_LO.index((kind, j)) + 1)

        def turn_bank(b, r, first):
            if isinstance(b, int) and b == 0:
                return f[r]
            return sp[spare(b - 1, ("turn", b, r), first)[0]]

        block = ctx.enter_context(nc.Block())

        @block.sync
        def _(sync):
            def load_rows(b, r, first):
                i = b * RT + r
                if not first:
                    sync.wait_ge(xt_turned, i - 3)
                sync.dma_start(xn[:, r, :], x[bass.ds(i * P, P), :]).then_inc(x_in[r], 16)

            def load_raw(kind, j):
                if j >= 2:
                    wait_split(sync, kind, j - 2)
                if kind == 2:
                    src = w2[j * P:j * P + hs(j), :]
                else:
                    src = (w1 if kind == 1 else w3)[:, DC * P * j:DC * P * j + DC * hs(j)]
                sync.dma_start(raw_tile(kind, j), src).then_inc(raw_in[raw_slot(kind, j)], 16)

            def load_residual(b):
                sync.dma_start(xres[:, :, :], xT[:, :, bass.ds(b * BLK, BLK)]).then_inc(res_in, 16)

            def store(b):
                for n, c in enumerate(OUT_ORDER):
                    sync.wait_ge(res_done, b * DC + n + 1)
                    sync.dma_start(outT[c * P:(c + 1) * P, bass.ds(b * BLK, BLK)], xres[:, c, :]).then_inc(out_done, 16)

            def rest(b, last):
                if not last:
                    for r in range(RT):
                        load_rows(b + 1, r, False)
                sync.wait_ge(out_done, b * (DC * 16))
                load_residual(b)
                store(b)

            load_rows(0, 0, True)
            sync.dma_start(lr[:, :], lora).then_inc(lora_in, 16)
            load_rows(0, 1, True)
            sync.dma_start(lane_c[:, :], lanes).then_inc(const_in, 16)
            load_raw(1, 0)
            load_rows(0, 2, True)
            load_rows(0, 3, True)
            load_raw(3, 0)
            sync.dma_start(spread[:, 0:LANES_ST], lora_st).then_inc(spread_in, 16)
            sync.dma_start(spread[:, LANES_ST:LANES_ST + LANES_MV], lora_mv).then_inc(spread_in, 16)
            for kind, j in FOLD_FIRST[2:]:
                load_raw(kind, j)
            sync.dma_start(lane_d[:, :], s4_lanes).then_inc(s4_in, 16)
            sync.dma_start(scal[:, :], s4_scalars.to_broadcast([P, 2])).then_inc(s4_in, 16)
            sync.dma_start(bp_sb[:, :], s4_bp).then_inc(bvec_in, 16)
            sync.dma_start(vc_sb[:, :], s4_vc).then_inc(bvec_in, 16)
            sync.dma_start(trig_sb[:, :, :].rearrange("p a l -> p (a l)"), trig.to_broadcast([P, 2 * D])).then_inc(s4_in, 16)
            load_raw(2, 1)
            sync.wait_ge(spread_lo, 1)
            for n, (st, mv) in enumerate(STACK):
                for hl, cols, lane_cols in ((st, slice(0, ST_COLS), slice(0, LANES_ST)),
                                            (mv, slice(ST_COLS, LORA_COLS), slice(LANES_ST, LANES_ST + LANES_MV))):
                    sync.dma_start(lst[n * R:(n + 1) * R, cols].bitcast(F32).rearrange("r (k c) -> r k c", k=P // R),
                                   spread_hl[:, hl, lane_cols].bitcast(F32)).then_inc(stack_in, 16)
            load_raw(1, 2)
            load_raw(3, 2)
            sync.dma_start(dft_sb[:, :, :], dft).then_inc(dft_in, 16)
            for kind, j in FOLDS[8:14]:
                load_raw(kind, j)
            for r in range(RT):
                load_rows(1, r, False)
            for kind, j in FOLDS[14:]:
                load_raw(kind, j)
            sync.wait_ge(fold_ready, len(FOLDS))
            load_residual(0)
            store(0)
            with sync.Fori(1, NBLK - 1) as b:
                rest(b, False)
            rest(NBLK - 1, True)
            sync.wait_ge(out_done, NBLK * DC * 16)

        @block.scalar
        def _(act):
            def fold_hi(kind, j):
                act.wait_ge(fold_added, FOLD_NO[kind, j] + 1)
                nc.scalar.copy(folded(kind, j, 0), raw_tile(kind, j)).then_inc(whi_done, 1)

            def rows_hi(b, r, par, first):
                i = b * RT + r
                act.wait_ge(xt_turned, i + 1)
                if first and r == 0 and b == 1:
                    act.wait_ge(wlo_done, len(DVE_LO))
                if not first:
                    act.wait_ge(conv_ready, (b - 1) * DC)
                nc.scalar.copy(xt[:, par, 0, :, r * P:(r + 1) * P],
                               turn_bank(b, r, first)[:, :].rearrange("p (c u) -> p c u", c=DC)).then_inc(xhi_done, 1)

            def hidden(b, j):
                t = b * HT + j
                act.wait_ge(h1_ready, t + 1)
                if not (isinstance(b, int) and t == 0):
                    act.wait_ge(glo_done, t)
                nc.scalar.activation(g[0:hs(j), :], h1[0:hs(j), :], ACT.Silu).then_inc(silu_done, 1)

            def hidden_hi(b, j):
                t = b * HT + j
                act.wait_ge(g_done, t + 1)
                if j > 0:
                    act.wait_ge(g_used, b * (HT - 1) + j)
                elif not isinstance(b, int) or b > 0:
                    act.wait_ge(f_ready, b * DC)
                nc.scalar.copy(ghl[0:hs(j), 0, :], g[0:hs(j), :]).then_inc(ghi_done, 1)

            def rows_norm(b, r):
                act.wait_ge(shift_ready, b * (RT // 2) + r // 2 + 1)
                nc.scalar.activation(xn[:, r, :], xn[:, r, :], ACT.Identity, bias=shift[:, r:r + 1],
                                     scale=rstd[:, r:r + 1]).then_inc(xn_ready, 1)

            def out_gate(b):
                for n, c in enumerate(OUT_ORDER):
                    e = b * DC + n
                    act.wait_ge(f_ready, e + 1)
                    if n >= 2:
                        act.wait_ge(res_done, e - 1)
                    elif not isinstance(b, int) or b > 0:
                        act.wait_ge(res_done, e - 1)
                    nc.scalar.activation(gate[:, n % 2, :], f[c][:, :], ACT.Silu).then_inc(gate_done, 1)

            def body(b, par_next, first, last):
                turn_at = TURN_AT_FIRST if first else TURN_AT
                for j in range(HT):
                    for place in ("gate", "up", "down"):
                        if place == "gate" and not (first and j == 0):
                            hidden(b, j)
                        if first:
                            for kind, t in folds(place, j):
                                fold_hi(kind, t)
                        if place == "up":
                            hidden_hi(b, j)
                        for r in () if last else turn_at.get((j, place), ()):
                            rows_hi(b + 1, r, par_next, first)
                        if not last and place == "down":
                            m = j - (5 if first else 0)
                            if m in (2, 4):
                                rows_norm(b + 1, m - 2)
                                rows_norm(b + 1, m - 1)
                        if first and (j, place) == KAPPA_AT:
                            act.wait_ge(kappa_ready, 1)
                            nc.scalar.copy(kap[:, :, :], sp[SPARE[("kappa",)][0]][:, 0:32].rearrange("p (c k) -> p c k", c=4)) \
                                .then_inc(kappa_copied, 1)
                            act.wait_ge(kappa_copied, 1)
                            act.sem_inc(spare_free[SPARE[("kappa",)][0]], 1)
                        if first and (j, place) == KROW_AT:
                            act.wait_ge(krow_ready, 1)
                            nc.scalar.copy(even_odd[:, :, :], sp[SPARE[("krow",)][0]][:, :].rearrange("p (a t) -> p a t", a=2)).then_inc(krow_copied, 1)
                            act.wait_ge(krow_copied, 1)
                            act.sem_inc(spare_free[SPARE[("krow",)][0]], 1)
                        if first and (j, place) == TOEPLITZ_AT:
                            act.wait_ge(tz_in, 16)
                            nc.scalar.copy(tzs[:, 0, :], tz[:, :]).then_inc(tz_hi, 1)
                if first:
                    for r in turn_at["out"]:
                        rows_hi(b + 1, r, par_next, first)
                out_gate(b)

            fold_hi(1, 0)
            rows_norm(0, 0)
            rows_norm(0, 1)
            rows_hi(0, 0, 0, True)
            rows_hi(0, 1, 0, True)
            rows_norm(0, 2)
            rows_norm(0, 3)
            fold_hi(3, 0)
            rows_hi(0, 2, 0, True)
            rows_hi(0, 3, 0, True)
            act.wait_ge(spread_in, 32)
            nc.scalar.copy(spread_hl[:, 0, :], spread[:, :]).then_inc(spread_hi, 1)
            fold_hi(1, 1)
            hidden(0, 0)
            fold_hi(3, 1)
            fold_hi(2, 0)
            act.wait_ge(b_ready, 1)
            nc.scalar.copy(bvec[:, :], sp[SPARE[("B",)][0]][:, 0:2]).then_inc(b_copied, 1)
            act.wait_ge(b_copied, 1)
            act.sem_inc(spare_free[SPARE[("B",)][0]], 1)
            body(0, 1, True, False)
            with act.Fori(1, NBLK - 1) as b:
                body(b, (b + 1) % 2, False, False)
            body(NBLK - 1, None, False, True)

        @block.vector
        def _(dve):
            def fold_add(kind, j):
                n = FOLD_NO[kind, j]
                bk, use = SPARE["fold", (kind, j)]
                dve.wait_ge(raw_in[raw_slot(kind, j)], 16 * (j // 2 + 1))
                dve.wait_ge(fold_ready, n + 1)
                rt = raw_tile(kind, j)
                nc.vector.scalar_tensor_tensor(out=rt, in0=sp[bk][0:rt.shape[0], 0:fold_cols(kind, j)],
                                               scalar=LORA_SCALE, in1=rt, op0=ALU.mult, op1=ALU.add) \
                    .then_inc(fold_added, 1)
                dve.wait_ge(fold_added, n + 1)
                dve.sem_inc(spare_free[bk], 1)

            def fold_lo(kind, j):
                if (kind, j) in POOL_LO:
                    return
                dve.wait_ge(whi_done, FOLD_NO[kind, j] + 1)
                nc.vector.tensor_tensor(folded(kind, j, 1), raw_tile(kind, j), folded(kind, j, 0).bitcast(F32),
                                        ALU.subtract).then_inc(wlo_done, 1)

            def rows_moments(b, r):
                i = b * RT + r
                dve.wait_ge(x_in[r], 16 * (b + 1))
                nc.vector.bn_stats(stats[:, r % 2, :], xn[:, r, :]).then_inc(stats_done, 1)
                dve.wait_ge(stats_done, i + 1)
                dve.sem_inc(stats_seen, 1)
                nc.vector.bn_aggr(moments[:, r, :], stats[:, r % 2, :]).then_inc(moments_ready, 1)

            def rows_lo(b, r, par, first):
                i = b * RT + r
                dve.wait_ge(xhi_done, i + 1)
                nc.vector.tensor_tensor(xt[:, par, 1, :, r * P:(r + 1) * P],
                                        turn_bank(b, r, first)[:, :].rearrange("p (c u) -> p c u", c=DC),
                                        xt[:, par, 0, :, r * P:(r + 1) * P].bitcast(F32),
                                        ALU.subtract).then_inc(xlo_done, 1)
                if not (isinstance(b, int) and b == 0):
                    dve.wait_ge(xlo_done, i + 1)
                    dve.sem_inc(spare_free[spare(b - 1, ("turn", b, r), first)[0]], 1)

            def hidden_mul(b, j):
                t = b * HT + j
                dve.wait_ge(silu_done, t + 1)
                dve.wait_ge(h3_ready, t + 1)
                nc.vector.tensor_tensor(g[0:hs(j), :], g[0:hs(j), :], h3[0:hs(j), :], ALU.mult).then_inc(g_done, 1)

            def hidden_lo(b, j):
                t = b * HT + j
                dve.wait_ge(ghi_done, t + 1)
                nc.vector.tensor_tensor(ghl[0:hs(j), 1, :], g[0:hs(j), :], ghl[0:hs(j), 0, :].bitcast(F32),
                                        ALU.subtract).then_inc(glo_done, 1)

            def out_sum(b):
                for n, c in enumerate(OUT_ORDER):
                    e = b * DC + n
                    dve.wait_ge(gate_done, e + 1)
                    dve.wait_ge(conv_ready, e + 1)
                    nc.vector.tensor_tensor(gate[:, n % 2, :], gate[:, n % 2, :], conv[c][:, :], ALU.mult) \
                        .then_inc(conv_used, 1)
                    dve.wait_ge(conv_used, e + 1)
                    if c < 2:
                        dve.sem_inc(spare_free[c], 1)
                    dve.wait_ge(res_in, 16 * (b + 1))
                    nc.vector.tensor_tensor(xres[:, c, :], xres[:, c, :], gate[:, n % 2, :], ALU.add) \
                        .then_inc(res_done, 1)

            def body(b, par_next, first, last):
                turn_at = TURN_AT_FIRST if first else TURN_AT
                for j in range(HT):
                    for place in ("gate", "up", "down"):
                        if place == "up" and not (first and j == 0):
                            hidden_mul(b, j)
                        if first:
                            for kind, t in folds(place, j):
                                fold_add(kind, t)
                                fold_lo(kind, t)
                        if place == "up":
                            hidden_lo(b, j)
                        if first and (j, place) in RECIPROCAL_AT:
                            n = RECIPROCAL_AT.index((j, place))
                            dve.wait_ge(mag_ready, 1)
                            part = mag[:, n * (D // 2):(n + 1) * (D // 2)]
                            nc.vector.reciprocal(part, part).then_inc(inv_ready, 1)
                        for r in () if last else turn_at.get((j, place), ()):
                            rows_lo(b + 1, r, par_next, first)
                        if not last and place == "down":
                            m = j - (5 if first else 0)
                            if 0 <= m < 4:
                                rows_moments(b + 1, m)
                if first:
                    for r in turn_at["out"]:
                        rows_lo(b + 1, r, par_next, first)
                out_sum(b)

            nc.vector.memset(g[:, :], 0.0).then_inc(g_cleared, 1)
            rows_moments(0, 0)
            rows_moments(0, 1)
            fold_add(1, 0)
            rows_moments(0, 2)
            rows_moments(0, 3)
            fold_lo(1, 0)
            rows_lo(0, 0, 0, True)
            rows_lo(0, 1, 0, True)
            fold_add(3, 0)
            rows_lo(0, 2, 0, True)
            rows_lo(0, 3, 0, True)
            fold_add(1, 1)
            fold_lo(1, 1)
            fold_add(3, 1)
            fold_lo(3, 1)
            hidden_mul(0, 0)
            fold_add(2, 0)
            fold_lo(2, 0)
            body(0, 1, True, False)
            with dve.Fori(1, NBLK - 1) as b:
                body(b, (b + 1) % 2, False, False)
            body(NBLK - 1, None, False, True)

        @block.tensor
        def _(pe):
            def take(b, use, first):
                bk, n = spare(b, use, first)
                if not isinstance(n, int) or n > 0:
                    pe.wait_ge(spare_free[bk], n)
                return sp[bk]

            def fold(kind, j):
                bankt = take(0, ("fold", (kind, j)), True)
                plain = j <= PLAIN[kind]
                a, bc = (A_FIRST[kind], FIRST_COLS[kind]) if plain else (A_COL[kind], B_COL[kind])
                fac = lr if plain else lst
                if (kind, j) == (1, PLAIN[1] + 1):
                    pe.wait_ge(stack_in, 2 * len(STACK) * 16)
                if kind == 2:
                    mm = pe.matmul(bankt[0:hs(j), :], fac[:, a + j * P:a + j * P + hs(j)], fac[:, bc:bc + D],
                                   start=True, stop=True)
                else:
                    for c in range(DC):
                        mm = pe.matmul(bankt[:, c * hs(j):(c + 1) * hs(j)], fac[:, a + c * P:a + (c + 1) * P],
                                       fac[:, bc + j * P:bc + j * P + hs(j)], start=True, stop=True)
                mm.then_inc(fold_ready, 1)

            def turn_rows(b, r, first):
                i = b * RT + r
                if isinstance(b, int) and b == 0:
                    bankt = f[r]
                else:
                    bankt = take(b - 1, ("turn", b, r), first)
                pe.wait_ge(xn_ready, i + 1)
                for c in range(DC):
                    mm = pe.transpose(bankt[:, c * P:(c + 1) * P], xn[:, r, c * P:(c + 1) * P], lane_c[:, CL:CL + P])
                mm.then_inc(xt_turned, 1)

            def three(out, w, m, start, stop):
                pe.matmul(out, w[1], m[0], start=start, stop=False)
                pe.matmul(out, w[0], m[1], start=False, stop=False)
                return pe.matmul(out, w[0], m[0], start=False, stop=stop)

            def hidden(b, par, j, kind, out, rows=slice(0, BLK)):
                for c in range(DC):
                    mm = three(out[0:hs(j), rows], [w13_tile(kind, j, hl)[:, c, :] for hl in (0, 1)],
                               [xt[:, par, hl, c, rows] for hl in (0, 1)], c == 0, c == DC - 1)
                return mm

            def keep_busy(n):
                for _ in range(n):
                    pe.matmul(h1[:, 0:P], g[:, 0:P], g[:, 0:P], start=True, stop=True)

            def start():
                lo, hi = slice(0, BLK // 2), slice(BLK // 2, BLK)
                pe.wait_ge(g_cleared, 1)
                keep_busy(7)
                pe.wait_ge(lora_in, 16)
                fold(1, 0)
                keep_busy(5)
                pe.wait_ge(const_in, 16)
                turn_rows(0, 0, True)
                turn_rows(0, 1, True)
                fold(3, 0)
                turn_rows(0, 2, True)
                wait_split(pe, 1, 0)
                pe.wait_ge(xlo_done, RT // 2)
                hidden(0, 0, 0, 1, h1, lo)
                turn_rows(0, 3, True)
                wait_split(pe, 3, 0)
                hidden(0, 0, 0, 3, h3, lo)
                fold(1, 1)
                pe.wait_ge(xlo_done, RT)
                hidden(0, 0, 0, 1, h1, hi).then_inc(h1_ready, 1)
                fold(3, 1)
                hidden(0, 0, 0, 3, h3, hi).then_inc(h3_ready, 1)
                fold(2, 0)
                bankt = take(0, ("B",), True)
                pe.wait_ge(bvec_in, 32)
                for ri in range(2):
                    mm = pe.matmul(bankt[:, ri:ri + 1], vc_sb[:, ri * P:(ri + 1) * P], bp_sb[:, :], start=True, stop=True)
                mm.then_inc(b_ready, 1)
                for place in ("gate", "up", "down"):
                    extras(0, 0, place, True, False)

            def down_wait(b, j):
                t = b * HT + j
                pe.wait_ge(ghi_done, t + 1)
                pe.wait_ge(glo_done, t + 1)
                if j == 0 and (not isinstance(b, int) or b > 0):
                    pe.wait_ge(gate_done, b * DC)

            def down_chunk(j, c):
                return three(f[c][:, :], [w2f[0:hs(j), j, hl, c * P:(c + 1) * P] for hl in (0, 1)],
                             [ghl[0:hs(j), hl, :] for hl in (0, 1)], j == 0, j == HT - 1)

            def down(b, j):
                down_wait(b, j)
                for c in range(DC):
                    mm = down_chunk(j, c)
                mm.then_inc(g_used, 1)

            def convolve(b, par, c_out, first):
                t = b * HT + HT
                if c_out < 2:
                    out = take(b, ("conv", b, c_out), first)
                else:
                    pe.wait_ge((g_done, silu_done)[c_out - 2], t)
                    out = conv[c_out]
                for c in range(c_out + 1):
                    k = (c_out - c) * P
                    mm = three(out[:, :], [tzs[:, hl, k:k + P] for hl in (0, 1)],
                               [xt[:, par, hl, c, :] for hl in (0, 1)], c == 0, c == c_out)
                mm.then_inc(conv_ready, 1)

            def extras(b, j, place, first, last):
                if first:
                    for kind, t in folds(place, j):
                        fold(kind, t)
                turn_at = TURN_AT_FIRST if first else TURN_AT
                for r in () if last else turn_at.get((j, place), ()):
                    turn_rows(b + 1, r, first)
                if first and (j, place) == KAPPA_AT:
                    bankt = take(0, ("kappa",), True)
                    pe.wait_ge(res_ready, 2)
                    pe.wait_ge(v_ready, 1)
                    for c in range(4):
                        mm = pe.matmul(bankt[:, 8 * c:8 * c + 8], res[:, c * P:(c + 1) * P], vmat[:, :], start=True, stop=True)
                    mm.then_inc(kappa_ready, 1)
                if first and (j, place) == KROW_AT:
                    bankt = take(0, ("krow",), True)
                    pe.wait_ge(dft_in, 16)
                    pe.wait_ge(coef_ready, 2)
                    for c in range(4):
                        half = slice(c // 2 * (D // 2), (c // 2 + 1) * (D // 2))
                        mm = pe.matmul(bankt[:, half], coef[:, c:c + 1].to_broadcast([P, P]), dft_sb[:, c, :],
                                       start=(c % 2 == 0), stop=(c % 2 == 1))
                    mm.then_inc(krow_ready, 1)

            def body(b, par, first, last):
                if first:
                    start()
                else:
                    pe.wait_ge(xlo_done, (b + 1) * RT)
                for j in range(1 if first else 0, HT):
                    t = b * HT + j
                    if first:
                        wait_split(pe, 1, j)
                    if j > 0:
                        pe.wait_ge(silu_done, t)
                    else:
                        pe.wait_ge(conv_used, (b - 1) * DC + 1)
                    hidden(b, par, j, 1, h1).then_inc(h1_ready, 1)
                    extras(b, j, "gate", first, last)
                    if first:
                        wait_split(pe, 3, j)
                    if j > 0:
                        pe.wait_ge(g_done, t)
                    else:
                        pe.wait_ge(conv_used, (b - 1) * DC + 2)
                    hidden(b, par, j, 3, h3).then_inc(h3_ready, 1)
                    extras(b, j, "up", first, last)
                    if j > 0:
                        if first:
                            wait_split(pe, 2, j - 1)
                        down(b, j - 1)
                    extras(b, j, "down", first, last)
                if first:
                    pe.wait_ge(tz_lo, 1)
                    wait_split(pe, 2, HT - 1)
                for n, c in enumerate(OUT_ORDER):
                    convolve(b, par, c, first)
                    if n == 0:
                        down_wait(b, HT - 1)
                    down_chunk(HT - 1, c).then_inc(f_ready, 1)
                    if n == 0 and first:
                        for r in TURN_AT_FIRST["out"]:
                            turn_rows(b + 1, r, first)

            body(0, 0, True, False)
            with pe.Fori(1, NBLK - 1) as b:
                body(b, b % 2, False, False)
            body(NBLK - 1, (NBLK - 1) % 2, False, True)

        @block.gpsimd
        def _(pool):
            steps = [0]

            def then(ins):
                steps[0] += 1
                ins.then_inc(s4_step, 1)
                pool.wait_ge(s4_step, steps[0])

            def ts(out, a, s1, s2, op0, op1=None):
                if op1 is None:
                    return nc.gpsimd.tensor_scalar(out, a, s1, None, op0)
                return nc.gpsimd.tensor_scalar(out, a, s1, s2, op0, op1)

            def tt(out, a, c, op):
                return nc.gpsimd.tensor_tensor(out, a, c, op)

            def rows_rstd(b, r):
                two, n = slice(r, r + 2), b * (RT // 2) + r // 2 + 1
                pool.wait_ge(moments_ready, b * RT + r + 2)
                tt(rstd[:, two], moments[:, two, 1], lane_c[:, 14:16], ALU.add).then_inc(eps_added, 1)
                pool.wait_ge(eps_added, n)
                tt(rstd[:, two], rstd[:, two], lane_c[:, 7:9], ALU.pow).then_inc(rstd_ready, 1)
                pool.wait_ge(rstd_ready, n)
                tt(shift[:, two], moments[:, two, 0], rstd[:, two], ALU.mult).then_inc(shift_step, 1)
                pool.wait_ge(shift_step, n)
                tt(shift[:, two], shift[:, two], lane_c[:, 10:12], ALU.mult).then_inc(shift_ready, 1)

            pool.wait_ge(const_in, 16)
            for r in range(0, RT, 2):
                rows_rstd(0, r)

            def fold_lo(kind, j):
                pool.wait_ge(whi_done, FOLD_NO[kind, j] + 1)
                tt(folded(kind, j, 1), raw_tile(kind, j), folded(kind, j, 0).bitcast(F32), ALU.subtract) \
                    .then_inc(wlo_pool, 1)
                pool.wait_ge(wlo_pool, POOL_LO.index((kind, j)) + 1)

            fold_lo(3, 0)
            pool.wait_ge(spread_hi, 1)
            tt(spread_hl[:, 1, :], spread[:, :], spread_hl[:, 0, :].bitcast(F32), ALU.subtract).then_inc(spread_lo, 1)
            pool.wait_ge(spread_lo, 1)
            fold_lo(3, 1)
            S, C = trig_sb[:, 0, :], trig_sb[:, 1, :]
            pool.wait_ge(s4_in, 16 * 3)
            then(ts(small[:, 1:2], scal[:, 1:2], -1.0, None, ALU.mult))
            then(tt(small[:, 2:3], lane_c[:, 9:10], small[:, 1:2], ALU.pow))
            then(ts(small[:, 2:3], small[:, 2:3], 2.0, None, ALU.mult))
            then(ts(small[:, 3:5], lane_d[:, 0:2], -1.0, None, ALU.mult))
            then(ts(den_re[:, :], C, small[:, 3:4], None, ALU.mult))
            then(ts(den_im[:, :], C, small[:, 4:5], None, ALU.mult))
            then(ts(res[:, :], S, small[:, 2:3], None, ALU.mult))
            then(tt(den_im[:, :], den_im[:, :], res[:, :], ALU.add))
            then(tt(mag[:, :], den_re[:, :], den_re[:, :], ALU.mult))
            then(tt(res[:, :], den_im[:, :], den_im[:, :], ALU.mult))
            tt(mag[:, :], mag[:, :], res[:, :], ALU.add).then_inc(mag_ready, 1)
            then(ts(vtmp[:, 0:1], lane_d[:, 3:4], lane_c[:, 6:7], None, ALU.mult))
            then(ts(vtmp[:, 1:2], lane_d[:, 5:6], lane_c[:, 6:7], None, ALU.mult))
            pool.wait_ge(b_copied, 1)
            v = vmat[:, :].rearrange("p (k r) -> p k r", r=2)
            for ui, (ua, ub) in enumerate([(lane_d[:, 4:5], vtmp[:, 1:2]), (lane_d[:, 2:3], vtmp[:, 0:1])]):
                for wi, (wre, wim) in enumerate([(bvec[:, 0:1], bvec[:, 1:2]), (lane_d[:, 6:7], lane_d[:, 7:8])]):
                    k = 2 * ui + wi
                    then(tt(vtmp[:, 4:5], ua, wre, ALU.mult))
                    then(tt(vtmp[:, 5:6], ub, wim, ALU.mult))
                    then(tt(v[:, k, 0:1], vtmp[:, 4:5], vtmp[:, 5:6], ALU.add))
                    then(tt(vtmp[:, 6:7], ua, wim, ALU.mult))
                    then(tt(vtmp[:, 7:8], ub, wre, ALU.mult))
                    ins = tt(v[:, k, 1:2], vtmp[:, 6:7], vtmp[:, 7:8], ALU.subtract)
                    if k == 3:
                        ins.then_inc(v_ready, 1)
                        pool.wait_ge(v_ready, 1)
                    else:
                        then(ins)
            pool.wait_ge(inv_ready, 2)
            then(ts(den_im[NS:P, :], den_im[NS:P, :], -1.0, None, ALU.mult))
            tt(res[0:NS, :], den_re[0:NS, :], mag[0:NS, :], ALU.mult).then_inc(res_ready, 1)
            pool.wait_ge(res_ready, 1)
            tt(res[NS:P, :], den_im[NS:P, :], mag[NS:P, :], ALU.mult).then_inc(res_ready, 1)
            pool.wait_ge(res_ready, 2)
            pool.wait_ge(kappa_copied, 1)
            k00, k01, k10, k11 = [(kap[:, :, 2 * k], kap[:, :, 2 * k + 1]) for k in range(4)]
            cosl = lane_c[:, 0:4]
            q = [cplx[:, i, :] for i in range(12)]

            def cmul(re, im, a, c, t0, t1):
                then(tt(t0, a[0], c[0], ALU.mult))
                then(tt(t1, a[1], c[1], ALU.mult))
                then(tt(re, t0, t1, ALU.subtract))
                then(tt(t0, a[0], c[1], ALU.mult))
                then(tt(t1, a[1], c[0], ALU.mult))
                then(tt(im, t0, t1, ALU.add))

            cmul(q[2], q[3], k01, k10, q[0], q[1])
            then(tt(q[2], q[2], cosl, ALU.mult))
            then(tt(q[3], q[3], cosl, ALU.mult))
            then(tt(q[4], k11[0], cosl, ALU.mult))
            then(ts(q[4], q[4], 1.0, None, ALU.add))
            then(tt(q[5], k11[1], cosl, ALU.mult))
            then(tt(q[6], q[4], q[4], ALU.mult))
            then(tt(q[7], q[5], q[5], ALU.mult))
            then(tt(q[6], q[6], q[7], ALU.add))
            then(tt(q[6], q[6], lane_c[:, 10:14], ALU.pow))
            then(tt(q[4], q[4], q[6], ALU.mult))
            then(tt(q[5], q[5], q[6], ALU.mult))
            then(ts(q[5], q[5], -1.0, None, ALU.mult))
            cmul(q[8], q[9], (q[2], q[3]), (q[4], q[5]), q[0], q[1])
            then(tt(q[8], k00[0], q[8], ALU.subtract))
            then(tt(q[9], k00[1], q[9], ALU.subtract))
            m = lane_c[:, 4:6]
            then(tt(q[0][:, 0:2], q[8][:, 2:4], m, ALU.mult))
            then(tt(q[1][:, 0:2], q[9][:, 0:2], m, ALU.mult))
            tt(coef[:, 0:2], q[8][:, 0:2], q[0][:, 0:2], ALU.subtract).then_inc(coef_ready, 1)
            tt(coef[:, 2:4], q[1][:, 0:2], q[9][:, 2:4], ALU.add).then_inc(coef_ready, 1)
            then(nc.gpsimd.memset(krow[:, 0:P], 0.0))
            pool.wait_ge(krow_copied, 1)
            then(tt(krow[:, P:P + D // 2], even_odd[:, 0, :], even_odd[:, 1, :], ALU.add))
            then(tt(krow[:, P + D - 1:P + D // 2 - 1:-1], even_odd[:, 0, :], even_odd[:, 1, :], ALU.subtract))
            tt(krow[:, P:P + 1], krow[:, P:P + 1], scal[:, 0:1], ALU.add).then_inc(krow_done, 1)
            pool.wait_ge(krow_done, 1)
            pool.dma_start(k_dram[:, :], krow[:, :]).then_inc(k_stored, 16)
            pool.wait_ge(k_stored, 16)
            shifted = bass.AP(tensor=k_dram, offset=P, ap=[[P + D - 1, P], [1, D]])
            pool.dma_start(tz[:, :], shifted).then_inc(tz_in, 16)
            rows_rstd(1, 0)
            pool.wait_ge(tz_hi, 1)
            tt(tzs[:, 1, :], tz[:, :], tzs[:, 0, :].bitcast(F32), ALU.subtract).then_inc(tz_lo, 1)
            rows_rstd(1, 2)
            with pool.Fori(1, NBLK - 1) as b:
                for r in range(0, RT, 2):
                    rows_rstd(b + 1, r)


def kernel(L0_attn_u, L0_attn_Lambda_ri, L0_attn_p_ri, L0_attn_q_ri, L0_attn_Vc_ri, L0_attn_Ct_ri, L0_attn_Bp,
           L0_attn_D, L0_attn_log_step, L0_ffn_w1, L0_ffn_w3, L0_ffn_w2, L0_ffn_lora_A1, L0_ffn_lora_B1,
           L0_ffn_lora_A3, L0_ffn_lora_B3, L0_ffn_lora_A2, L0_ffn_lora_B2):
    import numpy as _np
    import concourse.bacc as _bacc
    from concourse import mybir as _mybir
    from concourse.bass_utils import run_bass_kernel_spmd as _run

    c = _np.ascontiguousarray

    def turned_tiles(w):
        wt = _np.asarray(w).T.reshape(DC, P, HID)
        return _np.concatenate([wt[:, :, j * P:j * P + hs(j)].transpose(1, 0, 2).reshape(P, -1) for j in range(HT)], axis=1)

    x = _np.asarray(L0_attn_u).reshape(ROWS, D)
    lam, p, q = (_np.asarray(a) for a in (L0_attn_Lambda_ri, L0_attn_p_ri, L0_attn_q_ri))
    ct, vc = _np.asarray(L0_attn_Ct_ri).reshape(NS, 2), _np.asarray(L0_attn_Vc_ri)
    twice = lambda a: _np.concatenate([a, a])
    lanes_d = _np.stack([twice(lam[:, 0]), twice(lam[:, 1]),
                         _np.concatenate([q[:, 0], q[:, 1]]), _np.concatenate([q[:, 1], q[:, 0]]),
                         _np.concatenate([ct[:, 0], ct[:, 1]]), _np.concatenate([ct[:, 1], ct[:, 0]]),
                         twice(p[:, 0]), twice(p[:, 1])], axis=1)
    vct = vc.transpose(1, 2, 0)
    vct = _np.concatenate([vct[:, 0], vct[:, 0], vct[:, 1], vct[:, 1]], axis=1)
    a1, b1, a3, b3, a2, b2 = (_np.asarray(a) for a in (L0_ffn_lora_A1, L0_ffn_lora_B1, L0_ffn_lora_A3,
                                                      L0_ffn_lora_B3, L0_ffn_lora_A2, L0_ffn_lora_B2))
    lora_st = _np.concatenate([a1, a3, a2], axis=1)
    lora_mv = _np.concatenate([b1.T, b3.T, b2.T], axis=1)
    trig, lanes, dft = s4_constants()
    arrays = {
        "x": c(x), "xT": c(x.T.reshape(DC, P, ROWS).transpose(1, 0, 2)),
        "w1": c(turned_tiles(L0_ffn_w1)), "w3": c(turned_tiles(L0_ffn_w3)), "w2": c(_np.asarray(L0_ffn_w2).T),
        "lora": _np.concatenate([a1, a3, b1.T[:, :2 * P], b3.T[:, :2 * P], a2[:, :P], b2.T], axis=1),
         "lora_st": lora_st.reshape(P, LANES_ST),
        "lora_mv": lora_mv.reshape(P, LANES_MV), "s4_lanes": c(lanes_d), "s4_vc": c(vct), "s4_bp": c(_np.asarray(L0_attn_Bp)),
        "s4_scalars": c(_np.stack([_np.asarray(L0_attn_D), _np.asarray(L0_attn_log_step)], axis=1)),
        "trig": trig, "lanes": lanes, "dft": dft,
    }
    nc = _bacc.Bacc("TRN2", target_bir_lowering=False, num_devices=1)
    args = [nc.dram_tensor(f"{k}_dram", a.shape, _mybir.dt.from_np(a.dtype), kind="ExternalInput").ap()
            for k, a in arrays.items()]
    args.append(nc.dram_tensor("outT_dram", (D, ROWS), F32, kind="ExternalOutput").ap())
    build(nc, *args)
    r = _run(nc, [{f"{k}_dram": a for k, a in arrays.items()}], core_ids=[0])
    return r.results[0]["outT_dram"].T.reshape(2, 1024, D)
```

```python
from contextlib import ExitStack

import numpy as np
import concourse.bass as bass
from concourse import mybir

ALU = mybir.AluOpType
ACT = mybir.ActivationFunctionType
F32 = mybir.dt.float32
F32R = mybir.dt.float32r

P = 128
D = 512
HID = 1376
R = 16
LORA_SCALE = 2.0
ROWS = 2048
NS = 64
BLK = 512
NBLK = ROWS // BLK
RT = BLK // P
DC = D // P
HT = (HID + P - 1) // P
EPS = 1e-5
COS, MASK, SIGN, MINUS_HALF, EULER, MINUS_ONE, EPSILON, EYE = 0, 4, 6, 7, 9, 10, 14, 16
MINUS_LOG_STEP, TWO_OVER_STEP, MINUS_RE, MINUS_IM = 0, 1, 2, 3


def hs(j):
    return min(P, HID - j * P)


PAIRED_FROM = 3


def group(t):
    if t < PAIRED_FROM:
        return t, hs(t)
    t0 = t - (t - PAIRED_FROM) % 2
    return t0, hs(t0) + hs(t0 + 1)


def group_end(t):
    return t if t < PAIRED_FROM else group(t)[0] + 1


def part_chunks(t):
    if t < PAIRED_FROM:
        return range(DC)
    h = t - group(t)[0]
    return range(h * DC // 2, (h + 1) * DC // 2)


def part_cols(t):
    return len(part_chunks(t)) * group(t)[1]


PART_AT = [sum(part_cols(u) for u in range(t)) for t in range(HT)]


ST_COLS = 2 * D + HID
MV_COLS = 2 * HID + D
LORA_COLS = ST_COLS + MV_COLS
A_COL = {1: 0, 3: D, 2: 2 * D}
B_COL = {1: ST_COLS, 3: ST_COLS + HID, 2: ST_COLS + 2 * HID}
FIRST_COLS = {1: 2 * D, 3: 2 * D + 2 * P, 2: 2 * D + 5 * P}
LORA_FIRST = 3 * D + 5 * P
LANES_ST, LANES_MV = ST_COLS * R // P, MV_COLS * R // P
STACK = ((1, 0), (0, 1), (0, 0))
PLAIN = {1: 1, 3: 1, 2: 0}
A_FIRST = {1: 0, 3: D, 2: 2 * D + 4 * P}

FOLD_FIRST = [(1, 0), (3, 0), (1, 1), (3, 1), (2, 0)]


def folds(place, j):
    if j == 0 or j == HT - 1:
        return []
    if j == 1:
        return {"gate": [(1, 2)], "up": [(3, 2), (1, 3)], "down": [(2, 1), (3, 3)]}[place]
    if place == "down":
        return [(2, j)] if j < HT - 2 else [(2, HT - 2), (2, HT - 1)]
    return [(1 if place == "gate" else 3, j + 2)] if j < HT - 2 else []


FOLDS = FOLD_FIRST + [f for j in range(HT) for p in ("gate", "up", "down") for f in folds(p, j)]
FOLD_NO = {f: n for n, f in enumerate(FOLDS)}
POOL_LO = [(3, 1), (1, 3), (3, 3), (3, 4)]
DVE_LO = [f for f in FOLDS if f not in POOL_LO]

NORM_AT_FIRST = {(HT - 1, "up"): (0,), (HT - 1, "down"): (1,), "out": (2, 3)}
SPLIT_AT_FIRST = {(HT - 1, "down"): (0,), "out": (1, 2, 3)}
NORM_AT = {(5, "down"): (0,), (6, "down"): (1,), (7, "down"): (2,), (8, "down"): (3,), "out": ()}
SPLIT_AT = {(6, "down"): (0,), (7, "down"): (1,), (8, "down"): (2,), (9, "down"): (3,), "out": ()}

MOMENTS_AT_FIRST = {(4, "down"): (0,), (5, "down"): (1,), (6, "down"): (2, 3)}
MOMENTS_AT = {(r, "down"): (r,) for r in range(RT)}

RECIPROCAL_AT = [(2, "down"), (3, "down")]

KAPPA_AT, KROW_AT = (5, "gate"), (6, "down")
TOEPLITZ_AT = (8, "up")


def spare_uses():
    uses = [("fold", f) for f in FOLD_FIRST] + [("B",)]
    for j in range(HT):
        for place in ("gate", "up", "down"):
            uses += [("fold", f) for f in folds(place, j)]
            if (j, place) == KAPPA_AT:
                uses.append(("kappa",))
            if (j, place) == KROW_AT:
                uses.append(("krow",))
    return uses


def spare_table():
    table, count = {}, [0, 0]
    for n, use in enumerate(spare_uses()):
        table[use] = (n % 2, count[n % 2])
        count[n % 2] += 1
    for c in (0, 1):
        table["conv", 0, c] = (c, count[c])
    return table


SPARE = spare_table()


def spare(b, use, first):
    if first:
        return SPARE[use]
    bank, n = SPARE["conv", 0, use[2]]
    return bank, n + b


def s4_constants():
    L = D
    lane = np.arange(L // 2)
    mirror = np.where(lane == 0, L // 2, L - lane)
    l = np.concatenate([lane, mirror])
    half = np.pi * l / L
    trig = np.concatenate([np.sin(half), np.cos(half)])[None, :].astype(np.float32)
    cosc = np.cos(half).reshape(4, P).T
    mask = np.ones((P, 2))
    mask[0, 0] = 0.0
    sign = np.where(np.arange(P) < NS, 1.0, -1.0)[:, None]
    powers = np.tile([-0.5, -0.5, np.e, -1.0, -1.0, -1.0, -1.0, EPS, EPS], (P, 1))
    lanes = np.concatenate([cosc, mask, sign, powers, np.eye(P)], axis=1).astype(np.float32)
    t = np.arange(L // 2) + 0.5
    lc, ls = lane, np.where(lane == 0, L // 2, lane)
    cos_rows = np.cos(2 * np.pi * ((lc[:, None] * t[None, :]) % L) / L) / L
    sin_rows = -np.sin(2 * np.pi * ((ls[:, None] * t[None, :]) % L) / L) / L
    dft = np.concatenate([cos_rows, sin_rows]).reshape(4, P, L // 2).transpose(1, 0, 2).astype(np.float32)
    return trig, lanes, np.ascontiguousarray(dft)


def build(nc, x, xT, w1, w3, w2, lora, lora_st, lora_mv, s4_lanes, s4_vc, s4_bp, s4_scalars, trig, lanes, dft, outT):
    ctx = ExitStack()
    with ctx:
        base = (nc.sbuf_base + 63) // 64 * 64

        def at(name, shape, off, dt=F32):
            return nc.alloc_sbuf_tensor_at(name, shape, dt, offset=base + off)

        top = [0]

        def put(name, shape, dt=F32):
            off = (top[0] + 31) // 32 * 32
            top[0] = off + int(np.prod(shape[1:])) * 4
            return at(name, shape, off, dt)

        w13 = put("w13", [P, 4 * DC * HID], F32R)
        w2f_off = top[0]
        w2f = put("w2f", [P, HT, 2, D], F32R)
        xt_off = top[0]
        xt = put("xt", [P, 2, 2, DC, BLK], F32R)
        lora_off = top[0]
        lst = put("lora_stack", [len(STACK) * R, LORA_COLS], F32R)
        xn_off = top[0]
        xn = put("xn", [P, RT, D])
        g = put("g", [P, BLK])
        ghl = put("ghl", [P, 2, BLK], F32R)
        tz = put("tz", [P, D])
        tzs = put("tzs", [P, 2, D], F32R)
        lane_c = put("lane_c", [P, EYE + P])
        lane_d = put("lane_d", [P, 8])
        stats = put("stats", [P, 2, 6])
        moments = put("moments", [P, 4, 2])
        scales = put("scales", [P, 2, RT])
        bp_sb = put("bp_sb", [NS, 1])
        scal = put("scal", [P, 2])
        small = put("small", [P, 4])
        bvec = put("bvec", [P, 2])
        vmat = put("vmat", [P, 8])
        vtmp = put("vtmp", [P, 16])
        kap = put("kap", [P, 4, 8])
        cplx = put("cplx", [P, 12, 4])
        coef = put("coef", [P, 4])
        assert base + top[0] <= nc.sbuf_usable_end
        xnt = at("normal_rows", [P, 2, 2, DC, BLK], xt_off)
        raw = at("raw", [P, 6, BLK], xt_off + 2 * DC * BLK * 4)
        lr = at("lora_first", [R, LORA_FIRST], 7 * 4 * DC * P * 4)
        spread = at("lora_spread", [P, LANES_ST + LANES_MV], 4 * 4 * DC * P * 4)
        spread_hl = at("lora_spread_split", [P, 2, LANES_ST + LANES_MV], 5 * 4 * DC * P * 4, F32R)
        s4_tile = 5
        top[0] = w2f_off + s4_tile * 2 * D * 4
        trig_sb = put("trig_sb", [P, 2, D])
        den_re = put("den_re", [P, D])
        den_im = put("den_im", [P, D])
        mag = put("mag", [P, D])
        res = put("res", [P, D])
        dft_sb = put("dft_sb", [P, 4, D // 2])
        even_odd = put("even_odd", [P, 2, D // 2])
        vc_sb = put("vc_sb", [NS, 2 * P])
        krow = put("krow", [P, P + D])
        assert top[0] <= w2f_off + HT * 2 * D * 4
        xres = at("xres", [P, 2, (xn_off - lora_off) // 4], lora_off)
        gate = at("gate", [P, 2, BLK], lora_off + DC * BLK * 4)
        rows_next = at("rows_next", [P, 2, D], lora_off + (DC + 2) * BLK * 4)
        scale_rows = at("scale_rows", [P, 2, BLK], lora_off + (DC + 4) * BLK * 4)
        assert lora_off + (DC + 6) * BLK * 4 <= xn_off
        rows_tile = 9
        rows_1 = at("rows_1", [P, RT, D], rows_tile * 4 * DC * P * 4)

        k_dram = nc.dram_tensor("k_scratch", [P, P + D], F32, kind="Internal")
        scales_dram = nc.dram_tensor("scales_scratch", [2, BLK], F32, kind="Internal")

        def bank(name):
            return ctx.enter_context(nc.psum_tensor(name, [P, BLK], F32))

        h1, h3 = bank("h1"), bank("h3")
        sp = [bank("spare0"), bank("spare1")]
        f = [bank(f"f{i}") for i in range(DC)]
        conv = [sp[0], sp[1], h3, h1]
        OUT_ORDER = (3, 2, 1, 0)

        def sem(name):
            return ctx.enter_context(nc.semaphore(name))

        x_in = [sem(f"x_in{i}") for i in range(RT)]
        rows_in = [sem(f"rows_in{i}") for i in range(2)]
        raw_in = [sem(f"raw_in{i}") for i in range(6)]
        lora_in, const_in = sem("lora_in"), sem("const_in")
        spread_in, stack_in = sem("spread_in"), sem("stack_in")
        s4_in, bvec_in, dft_in = sem("s4_in"), sem("bvec_in"), sem("dft_in")
        res0_in, res_in = sem("res0_in"), sem("res_in")
        scale_rows_in, tz_in = sem("scale_rows_in"), sem("tz_in")
        out_done, scales_stored, k_stored = sem("out_done"), sem("scales_stored"), sem("k_stored")
        stats_done, stats_seen, moments_ready = sem("stats_done"), sem("stats_seen"), sem("moments_ready")
        eps_added, rstd_ready, shift_step, shift_ready = map(sem, ("eps_added", "rstd_ready", "shift_step", "shift_ready"))
        xn_ready, xt_turned = sem("xn_ready"), sem("xt_turned")
        scaled, normed = sem("scaled"), sem("normed")
        xhi_done, xlo_done = sem("xhi_done"), sem("xlo_done")
        fold_ready, fold_added, whi_done = sem("fold_ready"), sem("fold_added"), sem("whi_done")
        wlo_done, wlo_pool = sem("wlo_done"), sem("wlo_pool")
        spread_hi, spread_lo = sem("spread_hi"), sem("spread_lo")
        spare_free = [sem("spare_free0"), sem("spare_free1")]
        h1_ready, h3_ready, silu_done, g_done = map(sem, ("h1_ready", "h3_ready", "silu_done", "g_done"))
        ghi_done, glo_done, g_used = map(sem, ("ghi_done", "glo_done", "g_used"))
        g_cleared, table_loaded = sem("g_cleared"), sem("table_loaded")
        conv_ready, f_ready, gate_done, conv_used, res_done = map(
            sem, ("conv_ready", "f_ready", "gate_done", "conv_used", "res_done"))
        small_ready, den_ready, mag_ready, inv_ready, res_ready = map(
            sem, ("small_ready", "den_ready", "mag_ready", "inv_ready", "res_ready"))
        b_ready, b_copied, v_ready, kappa_ready, kappa_copied, coef_ready = map(
            sem, ("b_ready", "b_copied", "v_ready", "kappa_ready", "kappa_copied", "coef_ready"))
        krow_ready, krow_copied, krow_done, tz_hi, tz_lo = map(
            sem, ("krow_ready", "krow_copied", "krow_done", "tz_hi", "tz_lo"))
        s4_step = sem("s4_step")

        def w13_tile(kind, j, hl):
            t0, units = group(j)
            n = DC * units
            s = 4 * DC * P * t0 + ((kind // 2) * 2 + hl) * n
            u = (j - t0) * P
            return w13[:, s:s + n].rearrange("p (c u) -> p c u", c=DC)[:, :, u:u + hs(j)]

        def folded(kind, j, hl):
            if kind == 2:
                return w2f[0:hs(j), j, hl, :]
            t0, units = group(j)
            s = 4 * DC * P * t0 + ((kind // 2) * 2 + hl) * DC * units + part_chunks(j)[0] * units
            return w13[:, s:s + part_cols(j)]

        def raw_slot(kind, j):
            return (kind - 1) * 2 + j % 2

        def raw_tile(kind, j):
            s = raw_slot(kind, j)
            return raw[0:hs(j), s, :] if kind == 2 else raw[:, s, 0:part_cols(j)]

        def fold_cols(kind, j):
            return D if kind == 2 else part_cols(j)

        def wait_split(eng, kind, j):
            if (kind, j) in POOL_LO:
                eng.wait_ge(wlo_pool, POOL_LO.index((kind, j)) + 1)
            else:
                eng.wait_ge(wlo_done, DVE_LO.index((kind, j)) + 1)

        def resid(par, c):
            return xres[:, par, c * BLK:(c + 1) * BLK]

        def row_tile(b, r):
            if isinstance(b, int) and b < 2:
                return (xn, rows_1)[b][:, r, :]
            return rows_next[:, r % 2, :]

        def wait_residual(eng, b):
            if isinstance(b, int) and b == 0:
                eng.wait_ge(res0_in, 16)
            else:
                eng.wait_ge(res_in, 16 * b)

        def wait_group(eng, kind, j):
            for t in range(group(j)[0], group_end(j) + 1):
                wait_split(eng, kind, t)

        block = ctx.enter_context(nc.Block())

        @block.sync
        def _(sync):
            def load_rows(b, pair):
                src = x[bass.ds(b * BLK, BLK), :].rearrange("(p r) d -> p r d", r=RT)[:, 2 * pair:2 * pair + 2, :]
                if isinstance(b, int) and b < 2:
                    dst = rows_1[:, 2 * pair:2 * pair + 2, :]
                else:
                    sync.wait_ge(stats_done, b * RT + 2 * pair)
                    dst = rows_next[:, :, :]
                sync.dma_start(dst, src).then_inc(rows_in[pair], 16)

            def spread_scales(b):
                sync.wait_ge(shift_ready, (b + 1) * (RT // 2))
                sync.dma_start(scales_dram[:, :].rearrange("k (p r) -> p k r", r=RT), scales[:, :, :]) \
                    .then_inc(scales_stored, 16)
                sync.wait_ge(scales_stored, 16 * b)
                row = bass.AP(tensor=scales_dram, offset=0, ap=[[0, P], [BLK, 2], [1, BLK]])
                sync.dma_start(scale_rows[:, :, :], row).then_inc(scale_rows_in, 16)

            def load_raw(kind, j):
                if j >= 2:
                    wait_split(sync, kind, j - 2)
                if kind == 2:
                    src = w2[j * P:j * P + hs(j), :]
                else:
                    src = (w1 if kind == 1 else w3)[:, PART_AT[j]:PART_AT[j] + part_cols(j)]
                sync.dma_start(raw_tile(kind, j), src).then_inc(raw_in[raw_slot(kind, j)], 16)

            def load_residual(b, par):
                dst = xres[:, par, 0:DC * BLK].rearrange("p (c r) -> p c r", c=DC)
                src = xT[:, :, bass.ds(b * BLK, BLK)]
                sync.dma_start(dst, src).then_inc(res0_in if isinstance(b, int) and b == 0 else res_in, 16)

            def store(b, par):
                for n, c in enumerate(OUT_ORDER):
                    sync.wait_ge(res_done, b * DC + n + 1)
                    sync.dma_start(outT[c * P:(c + 1) * P, bass.ds(b * BLK, BLK)], resid(par, c)).then_inc(out_done, 16)

            def load_tile(r):
                sync.dma_start(xn[:, r, :], x[r * P:(r + 1) * P, :]).then_inc(x_in[r], 16)

            load_tile(0)
            sync.dma_start(lr[:, :], lora).then_inc(lora_in, 16)
            load_tile(1)
            sync.dma_start(lane_c[:, :], lanes).then_inc(const_in, 16)
            load_raw(1, 0)
            load_tile(2)
            load_tile(3)
            load_raw(3, 0)
            sync.dma_start(spread[:, 0:LANES_ST], lora_st).then_inc(spread_in, 16)
            sync.dma_start(spread[:, LANES_ST:LANES_ST + LANES_MV], lora_mv).then_inc(spread_in, 16)
            for kind, j in FOLD_FIRST[2:]:
                load_raw(kind, j)
            sync.dma_start(lane_d[:, :], s4_lanes).then_inc(s4_in, 16)
            sync.dma_start(scal[:, :], s4_scalars.to_broadcast([P, 2])).then_inc(s4_in, 16)
            sync.dma_start(bp_sb[:, :], s4_bp).then_inc(bvec_in, 16)
            sync.dma_start(vc_sb[:, :], s4_vc).then_inc(bvec_in, 16)
            sync.dma_start(trig_sb[:, :, :].rearrange("p a l -> p (a l)"), trig.to_broadcast([P, 2 * D])) \
                .then_inc(s4_in, 16)
            load_raw(2, 1)
            sync.wait_ge(spread_lo, 1)
            for n, (st, mv) in enumerate(STACK):
                for hl, cols, lane_cols in ((st, slice(0, ST_COLS), slice(0, LANES_ST)),
                                            (mv, slice(ST_COLS, LORA_COLS), slice(LANES_ST, LANES_ST + LANES_MV))):
                    sync.dma_start(lst[n * R:(n + 1) * R, cols].bitcast(F32).rearrange("r (k c) -> r k c", k=P // R),
                                   spread_hl[:, hl, lane_cols].bitcast(F32)).then_inc(stack_in, 16)
            early = [(1, 2), (3, 2), (1, 3), (3, 3)]
            for kind, j in early:
                load_raw(kind, j)
            sync.dma_start(dft_sb[:, :, :], dft).then_inc(dft_in, 16)
            later = [f_ for f_ in FOLDS[len(FOLD_FIRST):] if f_ not in early + [(2, 1)]]
            for kind, j in later[:6]:
                load_raw(kind, j)
            load_rows(1, 0)
            load_rows(1, 1)
            sync.wait_ge(xt_turned, RT)
            load_residual(1, 1)
            for kind, j in later[6:]:
                load_raw(kind, j)
            sync.wait_ge(fold_ready, len(FOLDS))
            spread_scales(1)
            load_residual(0, 0)
            store(0, 0)
            with sync.Fori(1, NBLK - 1) as b:
                load_rows(b + 1, 0)
                sync.wait_ge(out_done, b * (DC * 16))
                load_residual(b + 1, (b + 1) % 2)
                load_rows(b + 1, 1)
                spread_scales(b + 1)
                store(b, b % 2)
            store(NBLK - 1, (NBLK - 1) % 2)
            sync.wait_ge(out_done, NBLK * DC * 16)

        @block.scalar
        def _(act):
            def fold_hi(kind, j):
                act.wait_ge(fold_added, FOLD_NO[kind, j] + 1)
                if (kind, j) == (1, rows_tile):
                    act.wait_ge(stats_done, 2 * RT)
                nc.scalar.copy(folded(kind, j, 0), raw_tile(kind, j)).then_inc(whi_done, 1)

            def rows_hi(r):
                act.wait_ge(xt_turned, r + 1)
                nc.scalar.copy(xt[:, 0, 0, :, r * P:(r + 1) * P],
                               f[r][:, :].rearrange("p (c u) -> p c u", c=DC)).then_inc(xhi_done, 1)

            def next_hi(b, c, par):
                act.wait_ge(normed, (b - 1) * DC + c + 1)
                nc.scalar.copy(xt[:, par, 0, c, :], xnt[:, par, 1, c, :]).then_inc(xhi_done, 1)

            def hidden(b, j):
                t = b * HT + j
                act.wait_ge(h1_ready, t + 1)
                if not (isinstance(b, int) and t == 0):
                    act.wait_ge(glo_done, t)
                nc.scalar.activation(g[0:hs(j), :], h1[0:hs(j), :], ACT.Silu).then_inc(silu_done, 1)

            def hidden_hi(b, j):
                t = b * HT + j
                act.wait_ge(g_done, t + 1)
                if j > 0:
                    act.wait_ge(g_used, b * (HT - 1) + j)
                elif not isinstance(b, int) or b > 0:
                    act.wait_ge(f_ready, b * DC)
                nc.scalar.copy(ghl[0:hs(j), 0, :], g[0:hs(j), :]).then_inc(ghi_done, 1)

            def rows_norm(r):
                act.wait_ge(shift_ready, r // 2 + 1)
                nc.scalar.activation(xn[:, r, :], xn[:, r, :], ACT.Identity, bias=scales[:, 1, r:r + 1],
                                     scale=scales[:, 0, r:r + 1]).then_inc(xn_ready, 1)

            def out_gate(b):
                for n, c in enumerate(OUT_ORDER):
                    e = b * DC + n
                    act.wait_ge(f_ready, e + 1)
                    if n >= 2 or not isinstance(b, int) or b > 0:
                        act.wait_ge(res_done, e - 1)
                    nc.scalar.activation(gate[:, n % 2, :], f[c][:, :], ACT.Silu).then_inc(gate_done, 1)

            def body(b, par_next, first, last):
                norm_at = NORM_AT_FIRST if first else NORM_AT
                for j in range(HT):
                    for place in ("gate", "up", "down"):
                        if place == "gate" and not (first and j == 0):
                            hidden(b, j)
                        if first:
                            for kind, t in folds(place, j):
                                fold_hi(kind, t)
                        if place == "up":
                            hidden_hi(b, j)
                        for c in () if last else norm_at.get((j, place), ()):
                            next_hi(b + 1, c, par_next)
                        if first and (j, place) == (1, "gate"):
                            act.wait_ge(s4_in, 16 * 3)
                            act.wait_ge(small_ready, 1)
                            for out, trig_row, n in ((den_re, 1, MINUS_RE), (den_im, 1, MINUS_IM), (res, 0, TWO_OVER_STEP)):
                                nc.scalar.activation(out[:, :], trig_sb[:, trig_row, :], ACT.Identity,
                                                     scale=small[:, n:n + 1]).then_inc(den_ready, 1)
                        if first and (j, place) == KAPPA_AT:
                            act.wait_ge(kappa_ready, 1)
                            nc.scalar.copy(kap[:, :, :], sp[SPARE[("kappa",)][0]][:, 0:32].rearrange("p (c k) -> p c k", c=4)) \
                                .then_inc(kappa_copied, 1)
                            act.wait_ge(kappa_copied, 1)
                            act.sem_inc(spare_free[SPARE[("kappa",)][0]], 1)
                        if first and (j, place) == KROW_AT:
                            act.wait_ge(krow_ready, 1)
                            nc.scalar.copy(even_odd[:, :, :],
                                           sp[SPARE[("krow",)][0]][:, :].rearrange("p (a t) -> p a t", a=2)) \
                                .then_inc(krow_copied, 1)
                            act.wait_ge(krow_copied, 1)
                            act.sem_inc(spare_free[SPARE[("krow",)][0]], 1)
                        if first and (j, place) == TOEPLITZ_AT:
                            act.wait_ge(tz_in, 16)
                            nc.scalar.copy(tzs[:, 0, :], tz[:, :]).then_inc(tz_hi, 1)
                for c in () if last else norm_at["out"]:
                    next_hi(b + 1, c, par_next)
                out_gate(b)

            act.wait_ge(g_cleared, 1)
            nc.scalar.activation(g[:, P:P + 1], g[:, 0:1], ACT.Silu).then_inc(table_loaded, 1)
            rows_norm(0)
            rows_norm(1)
            fold_hi(1, 0)
            rows_hi(0)
            rows_hi(1)
            rows_norm(2)
            rows_norm(3)
            fold_hi(3, 0)
            rows_hi(2)
            rows_hi(3)
            act.wait_ge(spread_in, 32)
            nc.scalar.copy(spread_hl[:, 0, :], spread[:, :]).then_inc(spread_hi, 1)
            fold_hi(1, 1)
            hidden(0, 0)
            fold_hi(3, 1)
            fold_hi(2, 0)
            act.wait_ge(b_ready, 1)
            nc.scalar.copy(bvec[:, :], sp[SPARE[("B",)][0]][:, 0:2]).then_inc(b_copied, 1)
            act.wait_ge(b_copied, 1)
            act.sem_inc(spare_free[SPARE[("B",)][0]], 1)
            body(0, 1, True, False)
            with act.Fori(1, NBLK - 1) as b:
                body(b, (b + 1) % 2, False, False)
            body(NBLK - 1, None, False, True)

        @block.vector
        def _(dve):
            def fold_add(kind, j):
                n = FOLD_NO[kind, j]
                bk = SPARE["fold", (kind, j)][0]
                dve.wait_ge(raw_in[raw_slot(kind, j)], 16 * (j // 2 + 1))
                dve.wait_ge(fold_ready, n + 1)
                rt = raw_tile(kind, j)
                nc.vector.scalar_tensor_tensor(out=rt, in0=sp[bk][0:rt.shape[0], 0:fold_cols(kind, j)],
                                               scalar=LORA_SCALE, in1=rt, op0=ALU.mult, op1=ALU.add) \
                    .then_inc(fold_added, 1)
                dve.wait_ge(fold_added, n + 1)
                dve.sem_inc(spare_free[bk], 1)

            def fold_lo(kind, j):
                if (kind, j) in POOL_LO:
                    return
                dve.wait_ge(whi_done, FOLD_NO[kind, j] + 1)
                nc.vector.tensor_tensor(folded(kind, j, 1), raw_tile(kind, j), folded(kind, j, 0).bitcast(F32),
                                        ALU.subtract).then_inc(wlo_done, 1)

            def rows_moments(b, r):
                i = b * RT + r
                if isinstance(b, int) and b == 0:
                    dve.wait_ge(x_in[r], 16)
                else:
                    dve.wait_ge(rows_in[r // 2], 16 * b)
                nc.vector.bn_stats(stats[:, r % 2, :], row_tile(b, r)).then_inc(stats_done, 1)
                dve.wait_ge(stats_done, i + 1)
                dve.sem_inc(stats_seen, 1)
                nc.vector.bn_aggr(moments[:, r, :], stats[:, r % 2, :]).then_inc(moments_ready, 1)

            def rows_lo(r):
                dve.wait_ge(xhi_done, r + 1)
                nc.vector.tensor_tensor(xt[:, 0, 1, :, r * P:(r + 1) * P],
                                        f[r][:, :].rearrange("p (c u) -> p c u", c=DC),
                                        xt[:, 0, 0, :, r * P:(r + 1) * P].bitcast(F32),
                                        ALU.subtract).then_inc(xlo_done, 1)

            def next_shift(b, c, par):
                dve.wait_ge(scaled, (b - 1) * DC + c + 1)
                part = xnt[:, par, 1, c, :]
                nc.vector.tensor_tensor(part, part, scale_rows[:, 1, :], ALU.add).then_inc(normed, 1)

            def next_lo(b, c, par):
                dve.wait_ge(xhi_done, b * DC + c + 1)
                nc.vector.tensor_tensor(xt[:, par, 1, c, :], xnt[:, par, 1, c, :],
                                        xt[:, par, 0, c, :].bitcast(F32), ALU.subtract).then_inc(xlo_done, 1)

            def hidden_mul(b, j):
                t = b * HT + j
                dve.wait_ge(silu_done, t + 1)
                dve.wait_ge(h3_ready, t + 1)
                nc.vector.tensor_tensor(g[0:hs(j), :], g[0:hs(j), :], h3[0:hs(j), :], ALU.mult).then_inc(g_done, 1)

            def hidden_lo(b, j):
                t = b * HT + j
                dve.wait_ge(ghi_done, t + 1)
                nc.vector.tensor_tensor(ghl[0:hs(j), 1, :], g[0:hs(j), :], ghl[0:hs(j), 0, :].bitcast(F32),
                                        ALU.subtract).then_inc(glo_done, 1)

            def out_sum(b, par):
                for n, c in enumerate(OUT_ORDER):
                    e = b * DC + n
                    dve.wait_ge(gate_done, e + 1)
                    dve.wait_ge(conv_ready, e + 1)
                    nc.vector.tensor_tensor(gate[:, n % 2, :], gate[:, n % 2, :], conv[c][:, :], ALU.mult) \
                        .then_inc(conv_used, 1)
                    dve.wait_ge(conv_used, e + 1)
                    if c < 2:
                        dve.sem_inc(spare_free[c], 1)
                    wait_residual(dve, b)
                    nc.vector.tensor_tensor(resid(par, c), resid(par, c), gate[:, n % 2, :], ALU.add) \
                        .then_inc(res_done, 1)

            def body(b, par, par_next, first, last):
                norm_at = NORM_AT_FIRST if first else NORM_AT
                split_at = SPLIT_AT_FIRST if first else SPLIT_AT
                moments_at = MOMENTS_AT_FIRST if first else MOMENTS_AT
                late = []
                for j in range(HT):
                    for place in ("gate", "up", "down"):
                        if place == "up" and not (first and j == 0):
                            hidden_mul(b, j)
                        if first:
                            now = folds(place, j)
                            for f_ in late:
                                fold_lo(*f_)
                            for f_ in now:
                                fold_add(*f_)
                            for f_ in now[:-1]:
                                fold_lo(*f_)
                            late = now[-1:]
                        if place == "up":
                            hidden_lo(b, j)
                        if first and (j, place) in RECIPROCAL_AT:
                            n = RECIPROCAL_AT.index((j, place))
                            dve.wait_ge(mag_ready, 1)
                            part = mag[:, n * D // len(RECIPROCAL_AT):(n + 1) * D // len(RECIPROCAL_AT)]
                            nc.vector.reciprocal(part, part).then_inc(inv_ready, 1)
                        for c in () if last else norm_at.get((j, place), ()):
                            next_shift(b + 1, c, par_next)
                        for c in () if last else split_at.get((j, place), ()):
                            next_lo(b + 1, c, par_next)
                        for r in () if last else moments_at.get((j, place), ()):
                            rows_moments(b + 1, r)
                if not last:
                    for c in norm_at["out"]:
                        next_shift(b + 1, c, par_next)
                    for c in split_at["out"]:
                        next_lo(b + 1, c, par_next)
                out_sum(b, par)

            nc.vector.memset(g[:, 0:P], 0.0).then_inc(g_cleared, 1)
            rows_moments(0, 0)
            rows_moments(0, 1)
            rows_moments(0, 2)
            fold_add(1, 0)
            rows_moments(0, 3)
            fold_lo(1, 0)
            rows_lo(0)
            rows_lo(1)
            fold_add(3, 0)
            fold_lo(3, 0)
            rows_lo(2)
            rows_lo(3)
            fold_add(1, 1)
            fold_lo(1, 1)
            fold_add(3, 1)
            fold_lo(3, 1)
            hidden_mul(0, 0)
            fold_add(2, 0)
            fold_lo(2, 0)
            body(0, 0, 1, True, False)
            with dve.Fori(1, NBLK - 1) as b:
                body(b, b % 2, (b + 1) % 2, False, False)
            body(NBLK - 1, (NBLK - 1) % 2, None, False, True)

        @block.tensor
        def _(pe):
            def take(b, use, first):
                bk, n = spare(b, use, first)
                if not isinstance(n, int) or n > 0:
                    pe.wait_ge(spare_free[bk], n)
                return sp[bk]

            def fold(kind, j):
                bankt = take(0, ("fold", (kind, j)), True)
                plain = j <= PLAIN[kind]
                a, bc = (A_FIRST[kind], FIRST_COLS[kind]) if plain else (A_COL[kind], B_COL[kind])
                fac = lr if plain else lst
                if (kind, j) == (1, PLAIN[1] + 1):
                    pe.wait_ge(stack_in, 2 * len(STACK) * 16)
                if kind == 2:
                    mm = pe.matmul(bankt[0:hs(j), :], fac[:, a + j * P:a + j * P + hs(j)], fac[:, bc:bc + D],
                                   start=True, stop=True)
                else:
                    t0, units = group(j)
                    for n, c in enumerate(part_chunks(j)):
                        mm = pe.matmul(bankt[:, n * units:(n + 1) * units], fac[:, a + c * P:a + (c + 1) * P],
                                       fac[:, bc + t0 * P:bc + t0 * P + units], start=True, stop=True)
                mm.then_inc(fold_ready, 1)

            def turn_rows(r):
                pe.wait_ge(xn_ready, r + 1)
                for c in range(DC):
                    mm = pe.transpose(f[r][:, c * P:(c + 1) * P], xn[:, r, c * P:(c + 1) * P], lane_c[:, EYE:EYE + P])
                mm.then_inc(xt_turned, 1)

            def three(out, w, m, start, stop):
                pe.matmul(out, w[1], m[0], start=start, stop=False)
                pe.matmul(out, w[0], m[1], start=False, stop=False)
                return pe.matmul(out, w[0], m[0], start=False, stop=stop)

            def hidden(b, par, j, kind, out, rows=slice(0, BLK)):
                for c in range(DC):
                    if j == 0 and kind == 1 and not (isinstance(b, int) and b == 0):
                        pe.wait_ge(xlo_done, b * DC + c + 1)
                    mm = three(out[0:hs(j), rows], [w13_tile(kind, j, hl)[:, c, :] for hl in (0, 1)],
                               [xt[:, par, hl, c, rows] for hl in (0, 1)], c == 0, c == DC - 1)
                return mm

            def keep_busy(n):
                for _ in range(n):
                    pe.matmul(h1[:, 0:P], g[:, 0:P], g[:, 0:P], start=True, stop=True)

            def start():
                lo, hi = slice(0, BLK // 2), slice(BLK // 2, BLK)
                pe.wait_ge(g_cleared, 1)
                keep_busy(7)
                pe.wait_ge(lora_in, 16)
                fold(1, 0)
                fold(3, 0)
                keep_busy(1)
                pe.wait_ge(const_in, 16)
                turn_rows(0)
                turn_rows(1)
                keep_busy(2)
                pe.wait_ge(whi_done, 1)
                pe.wait_ge(xhi_done, RT // 2)
                for c in range(DC):
                    pe.matmul(h1[:, lo], w13_tile(1, 0, 0)[:, c, :], xt[:, 0, 0, c, lo], start=(c == 0), stop=False)
                wait_split(pe, 1, 0)
                pe.wait_ge(xlo_done, RT // 2)
                for c in range(DC):
                    pe.matmul(h1[:, lo], w13_tile(1, 0, 1)[:, c, :], xt[:, 0, 0, c, lo], start=False, stop=False)
                    pe.matmul(h1[:, lo], w13_tile(1, 0, 0)[:, c, :], xt[:, 0, 1, c, lo], start=False, stop=(c == DC - 1))
                turn_rows(2)
                turn_rows(3)
                wait_split(pe, 3, 0)
                hidden(0, 0, 0, 3, h3, lo)
                fold(1, 1)
                pe.wait_ge(xlo_done, RT)
                hidden(0, 0, 0, 1, h1, hi).then_inc(h1_ready, 1)
                fold(3, 1)
                hidden(0, 0, 0, 3, h3, hi).then_inc(h3_ready, 1)
                fold(2, 0)
                bankt = take(0, ("B",), True)
                pe.wait_ge(bvec_in, 32)
                for ri in range(2):
                    mm = pe.matmul(bankt[:, ri:ri + 1], vc_sb[:, ri * P:(ri + 1) * P], bp_sb[:, :], start=True, stop=True)
                mm.then_inc(b_ready, 1)

            def down_wait(b, j):
                t = b * HT + j
                pe.wait_ge(ghi_done, t + 1)
                pe.wait_ge(glo_done, t + 1)
                if j == 0 and (not isinstance(b, int) or b > 0):
                    pe.wait_ge(gate_done, b * DC)

            def down_chunk(j, c):
                return three(f[c][:, :], [w2f[0:hs(j), j, hl, c * P:(c + 1) * P] for hl in (0, 1)],
                             [ghl[0:hs(j), hl, :] for hl in (0, 1)], j == 0, j == HT - 1)

            def down(b, j):
                down_wait(b, j)
                for c in range(DC):
                    mm = down_chunk(j, c)
                mm.then_inc(g_used, 1)

            def convolve(b, par, c_out, first):
                t = b * HT + HT
                if c_out < 2:
                    out = take(b, ("conv", b, c_out), first)
                else:
                    pe.wait_ge((g_done, silu_done)[c_out - 2], t)
                    out = conv[c_out]
                for c in range(c_out + 1):
                    k = (c_out - c) * P
                    mm = three(out[:, :], [tzs[:, hl, k:k + P] for hl in (0, 1)],
                               [xt[:, par, hl, c, :] for hl in (0, 1)], c == 0, c == c_out)
                mm.then_inc(conv_ready, 1)

            def extras(j, place):
                for kind, t in folds(place, j):
                    fold(kind, t)
                if (j, place) == KAPPA_AT:
                    bankt = take(0, ("kappa",), True)
                    pe.wait_ge(res_ready, 2)
                    pe.wait_ge(v_ready, 1)
                    for c in range(4):
                        mm = pe.matmul(bankt[:, 8 * c:8 * c + 8], res[:, c * P:(c + 1) * P], vmat[:, :],
                                       start=True, stop=True)
                    mm.then_inc(kappa_ready, 1)
                if (j, place) == KROW_AT:
                    bankt = take(0, ("krow",), True)
                    pe.wait_ge(dft_in, 16)
                    pe.wait_ge(coef_ready, 2)
                    for c in range(4):
                        half = slice(c // 2 * (D // 2), (c // 2 + 1) * (D // 2))
                        mm = pe.matmul(bankt[:, half], coef[:, c:c + 1].to_broadcast([P, P]), dft_sb[:, c, :],
                                       start=(c % 2 == 0), stop=(c % 2 == 1))
                    mm.then_inc(krow_ready, 1)

            def body(b, par, first):
                if first:
                    start()
                for j in range(1 if first else 0, HT):
                    t = b * HT + j
                    if first:
                        wait_group(pe, 1, j)
                    if j > 0:
                        pe.wait_ge(silu_done, t)
                    else:
                        pe.wait_ge(conv_used, (b - 1) * DC + 1)
                    hidden(b, par, j, 1, h1).then_inc(h1_ready, 1)
                    if first:
                        extras(j, "gate")
                    if first:
                        wait_group(pe, 3, j)
                    if j > 0:
                        pe.wait_ge(g_done, t)
                    else:
                        pe.wait_ge(conv_used, (b - 1) * DC + 2)
                    hidden(b, par, j, 3, h3).then_inc(h3_ready, 1)
                    if first:
                        extras(j, "up")
                    if j > 0:
                        if first:
                            wait_split(pe, 2, j - 1)
                        down(b, j - 1)
                    if first:
                        extras(j, "down")
                if first:
                    pe.wait_ge(tz_lo, 1)
                    wait_split(pe, 2, HT - 1)
                for n, c in enumerate(OUT_ORDER):
                    if n < DC - 1:
                        convolve(b, par, c, first)
                    if n == 0:
                        down_wait(b, HT - 1)
                    down_chunk(HT - 1, c).then_inc(f_ready, 1)
                    if n == DC - 1:
                        convolve(b, par, c, first)

            body(0, 0, True)
            with pe.Fori(1, NBLK) as b:
                body(b, b % 2, False)

        @block.gpsimd
        def _(pool):
            steps = [0]

            def then(ins):
                steps[0] += 1
                ins.then_inc(s4_step, 1)
                pool.wait_ge(s4_step, steps[0])

            def ts(out, a, scalar, op):
                return nc.gpsimd.tensor_scalar(out, a, scalar, None, op)

            def tt(out, a, c, op):
                return nc.gpsimd.tensor_tensor(out, a, c, op)

            def rows_rstd(b, r):
                two, n = slice(r, r + 2), b * (RT // 2) + r // 2 + 1
                pool.wait_ge(moments_ready, b * RT + r + 2)
                tt(scales[:, 0, two], moments[:, two, 1], lane_c[:, EPSILON:EPSILON + 2], ALU.add).then_inc(eps_added, 1)
                pool.wait_ge(eps_added, n)
                tt(scales[:, 0, two], scales[:, 0, two], lane_c[:, MINUS_HALF:MINUS_HALF + 2], ALU.pow) \
                    .then_inc(rstd_ready, 1)
                pool.wait_ge(rstd_ready, n)
                tt(scales[:, 1, two], moments[:, two, 0], scales[:, 0, two], ALU.mult).then_inc(shift_step, 1)
                pool.wait_ge(shift_step, n)
                tt(scales[:, 1, two], scales[:, 1, two], lane_c[:, MINUS_ONE:MINUS_ONE + 2], ALU.mult) \
                    .then_inc(shift_ready, 1)

            def next_scale(b, par):
                pool.wait_ge(scale_rows_in, 16 * b)
                pool.wait_ge(res_in, 16 * b)
                for c in range(DC):
                    tt(xnt[:, par, 1, c, :], resid(par, c), scale_rows[:, 0, :], ALU.mult).then_inc(scaled, 1)

            pool.wait_ge(const_in, 16)
            for r in range(0, RT, 2):
                rows_rstd(0, r)

            def fold_lo(kind, j):
                pool.wait_ge(whi_done, FOLD_NO[kind, j] + 1)
                tt(folded(kind, j, 1), raw_tile(kind, j), folded(kind, j, 0).bitcast(F32), ALU.subtract) \
                    .then_inc(wlo_pool, 1)
                pool.wait_ge(wlo_pool, POOL_LO.index((kind, j)) + 1)

            pool.wait_ge(spread_hi, 1)
            tt(spread_hl[:, 1, :], spread[:, :], spread_hl[:, 0, :].bitcast(F32), ALU.subtract).then_inc(spread_lo, 1)
            pool.wait_ge(spread_lo, 1)
            fold_lo(3, 1)
            pool.wait_ge(s4_in, 16 * 3)
            then(ts(small[:, MINUS_LOG_STEP:MINUS_LOG_STEP + 1], scal[:, 1:2], -1.0, ALU.mult))
            then(tt(small[:, TWO_OVER_STEP:TWO_OVER_STEP + 1], lane_c[:, EULER:EULER + 1],
                    small[:, MINUS_LOG_STEP:MINUS_LOG_STEP + 1], ALU.pow))
            then(ts(small[:, TWO_OVER_STEP:TWO_OVER_STEP + 1], small[:, TWO_OVER_STEP:TWO_OVER_STEP + 1], 2.0, ALU.mult))
            then(ts(small[:, MINUS_RE:MINUS_IM + 1], lane_d[:, 0:2], -1.0, ALU.mult))
            pool.sem_inc(small_ready, 1)
            pool.wait_ge(den_ready, 3)
            then(tt(den_im[:, :], den_im[:, :], res[:, :], ALU.add))
            then(tt(mag[:, :], den_re[:, :], den_re[:, :], ALU.mult))
            then(tt(res[:, :], den_im[:, :], den_im[:, :], ALU.mult))
            tt(mag[:, :], mag[:, :], res[:, :], ALU.add).then_inc(mag_ready, 1)
            for kind, j in POOL_LO[1:]:
                fold_lo(kind, j)
            then(ts(vtmp[:, 0:1], lane_d[:, 3:4], lane_c[:, SIGN:SIGN + 1], ALU.mult))
            then(ts(vtmp[:, 1:2], lane_d[:, 5:6], lane_c[:, SIGN:SIGN + 1], ALU.mult))
            pool.wait_ge(b_copied, 1)
            v = vmat[:, :].rearrange("p (k r) -> p k r", r=2)
            for ui, (ua, ub) in enumerate([(lane_d[:, 4:5], vtmp[:, 1:2]), (lane_d[:, 2:3], vtmp[:, 0:1])]):
                for wi, (wre, wim) in enumerate([(bvec[:, 0:1], bvec[:, 1:2]), (lane_d[:, 6:7], lane_d[:, 7:8])]):
                    k = 2 * ui + wi
                    then(tt(vtmp[:, 4:5], ua, wre, ALU.mult))
                    then(tt(vtmp[:, 5:6], ub, wim, ALU.mult))
                    then(tt(v[:, k, 0:1], vtmp[:, 4:5], vtmp[:, 5:6], ALU.add))
                    then(tt(vtmp[:, 6:7], ua, wim, ALU.mult))
                    then(tt(vtmp[:, 7:8], ub, wre, ALU.mult))
                    then(tt(v[:, k, 1:2], vtmp[:, 6:7], vtmp[:, 7:8], ALU.subtract))
            ts(vmat[:, :], vmat[:, :], lane_c[:, SIGN:SIGN + 1], ALU.mult).then_inc(v_ready, 1)
            pool.wait_ge(v_ready, 1)
            pool.wait_ge(inv_ready, len(RECIPROCAL_AT))
            tt(res[0:NS, :], den_re[0:NS, :], mag[0:NS, :], ALU.mult).then_inc(res_ready, 1)
            pool.wait_ge(res_ready, 1)
            tt(res[NS:P, :], den_im[NS:P, :], mag[NS:P, :], ALU.mult).then_inc(res_ready, 1)
            pool.wait_ge(res_ready, 2)
            pool.wait_ge(kappa_copied, 1)
            k00, k01, k10, k11 = [(kap[:, :, 2 * k], kap[:, :, 2 * k + 1]) for k in range(4)]
            cosl = lane_c[:, COS:COS + 4]
            q = [cplx[:, i, :] for i in range(12)]

            def cmul(re, im, a, c, t0, t1):
                then(tt(t0, a[0], c[0], ALU.mult))
                then(tt(t1, a[1], c[1], ALU.mult))
                then(tt(re, t0, t1, ALU.subtract))
                then(tt(t0, a[0], c[1], ALU.mult))
                then(tt(t1, a[1], c[0], ALU.mult))
                then(tt(im, t0, t1, ALU.add))

            cmul(q[2], q[3], k01, k10, q[0], q[1])
            then(tt(q[2], q[2], cosl, ALU.mult))
            then(tt(q[3], q[3], cosl, ALU.mult))
            then(tt(q[4], k11[0], cosl, ALU.mult))
            then(ts(q[4], q[4], 1.0, ALU.add))
            then(tt(q[5], k11[1], cosl, ALU.mult))
            then(tt(q[6], q[4], q[4], ALU.mult))
            then(tt(q[7], q[5], q[5], ALU.mult))
            then(tt(q[6], q[6], q[7], ALU.add))
            then(tt(q[6], q[6], lane_c[:, MINUS_ONE:MINUS_ONE + 4], ALU.pow))
            then(tt(q[4], q[4], q[6], ALU.mult))
            then(tt(q[5], q[5], q[6], ALU.mult))
            then(ts(q[5], q[5], -1.0, ALU.mult))
            cmul(q[8], q[9], (q[2], q[3]), (q[4], q[5]), q[0], q[1])
            then(tt(q[8], k00[0], q[8], ALU.subtract))
            then(tt(q[9], k00[1], q[9], ALU.subtract))
            m = lane_c[:, MASK:MASK + 2]
            then(tt(q[0][:, 0:2], q[8][:, 2:4], m, ALU.mult))
            then(tt(q[1][:, 0:2], q[9][:, 0:2], m, ALU.mult))
            tt(coef[:, 0:2], q[8][:, 0:2], q[0][:, 0:2], ALU.subtract).then_inc(coef_ready, 1)
            tt(coef[:, 2:4], q[1][:, 0:2], q[9][:, 2:4], ALU.add).then_inc(coef_ready, 1)
            then(nc.gpsimd.memset(krow[:, 0:P], 0.0))
            pool.wait_ge(krow_copied, 1)
            then(tt(krow[:, P:P + D // 2], even_odd[:, 0, :], even_odd[:, 1, :], ALU.add))
            then(tt(krow[:, P + D - 1:P + D // 2 - 1:-1], even_odd[:, 0, :], even_odd[:, 1, :], ALU.subtract))
            tt(krow[:, P:P + 1], krow[:, P:P + 1], scal[:, 0:1], ALU.add).then_inc(krow_done, 1)
            pool.wait_ge(krow_done, 1)
            pool.dma_start(k_dram[:, :], krow[:, :]).then_inc(k_stored, 16)
            pool.wait_ge(k_stored, 16)
            shifted = bass.AP(tensor=k_dram, offset=P, ap=[[P + D - 1, P], [1, D]])
            pool.dma_start(tz[:, :], shifted).then_inc(tz_in, 16)
            pool.wait_ge(xn_ready, RT)
            rows_rstd(1, 0)
            pool.wait_ge(tz_hi, 1)
            tt(tzs[:, 1, :], tz[:, :], tzs[:, 0, :].bitcast(F32), ALU.subtract).then_inc(tz_lo, 1)
            rows_rstd(1, 2)
            pool.wait_ge(wlo_done, len(DVE_LO))
            next_scale(1, 1)
            with pool.Fori(1, NBLK - 1) as b:
                for r in range(0, RT, 2):
                    rows_rstd(b + 1, r)
                pool.wait_ge(conv_ready, b * DC)
                next_scale(b + 1, (b + 1) % 2)


def kernel(L0_attn_u, L0_attn_Lambda_ri, L0_attn_p_ri, L0_attn_q_ri, L0_attn_Vc_ri, L0_attn_Ct_ri, L0_attn_Bp,
           L0_attn_D, L0_attn_log_step, L0_ffn_w1, L0_ffn_w3, L0_ffn_w2, L0_ffn_lora_A1, L0_ffn_lora_B1,
           L0_ffn_lora_A3, L0_ffn_lora_B3, L0_ffn_lora_A2, L0_ffn_lora_B2):
    import numpy as _np
    import concourse.bacc as _bacc
    from concourse import mybir as _mybir
    from concourse.bass_utils import run_bass_kernel_spmd as _run

    c = _np.ascontiguousarray

    def turned_tiles(w):
        wt = _np.asarray(w).T.reshape(DC, P, HID)
        parts = [wt[part_chunks(t)[0]:part_chunks(t)[-1] + 1, :, group(t)[0] * P:group(t)[0] * P + group(t)[1]]
                 for t in range(HT)]
        return _np.concatenate([p_.transpose(1, 0, 2).reshape(P, -1) for p_ in parts], axis=1)

    x = _np.asarray(L0_attn_u).reshape(ROWS, D)
    lam, p, q = (_np.asarray(a) for a in (L0_attn_Lambda_ri, L0_attn_p_ri, L0_attn_q_ri))
    ct, vc = _np.asarray(L0_attn_Ct_ri).reshape(NS, 2), _np.asarray(L0_attn_Vc_ri)
    twice = lambda a: _np.concatenate([a, a])
    lanes_d = _np.stack([twice(lam[:, 0]), twice(lam[:, 1]),
                         _np.concatenate([q[:, 0], q[:, 1]]), _np.concatenate([q[:, 1], q[:, 0]]),
                         _np.concatenate([ct[:, 0], ct[:, 1]]), _np.concatenate([ct[:, 1], ct[:, 0]]),
                         twice(p[:, 0]), twice(p[:, 1])], axis=1)
    vct = vc.transpose(1, 2, 0)
    vct = _np.concatenate([vct[:, 0], vct[:, 0], vct[:, 1], vct[:, 1]], axis=1)
    a1, b1, a3, b3, a2, b2 = (_np.asarray(a) for a in (L0_ffn_lora_A1, L0_ffn_lora_B1, L0_ffn_lora_A3,
                                                      L0_ffn_lora_B3, L0_ffn_lora_A2, L0_ffn_lora_B2))
    lora_st = _np.concatenate([a1, a3, a2], axis=1)
    lora_mv = _np.concatenate([b1.T, b3.T, b2.T], axis=1)
    trig, lanes, dft = s4_constants()
    arrays = {
        "x": c(x), "xT": c(x.T.reshape(DC, P, ROWS).transpose(1, 0, 2)),
        "w1": c(turned_tiles(L0_ffn_w1)), "w3": c(turned_tiles(L0_ffn_w3)), "w2": c(_np.asarray(L0_ffn_w2).T),
        "lora": _np.concatenate([a1, a3, b1.T[:, :2 * P], b3.T[:, :2 * P], a2[:, :P], b2.T], axis=1),
        "lora_st": lora_st.reshape(P, LANES_ST),
        "lora_mv": lora_mv.reshape(P, LANES_MV),
        "s4_lanes": c(lanes_d), "s4_vc": c(vct), "s4_bp": c(_np.asarray(L0_attn_Bp)),
        "s4_scalars": c(_np.stack([_np.asarray(L0_attn_D), _np.asarray(L0_attn_log_step)], axis=1)),
        "trig": trig, "lanes": lanes, "dft": dft,
    }
    nc = _bacc.Bacc("TRN2", target_bir_lowering=False, num_devices=1)
    args = [nc.dram_tensor(f"{k}_dram", a.shape, _mybir.dt.from_np(a.dtype), kind="ExternalInput").ap()
            for k, a in arrays.items()]
    args.append(nc.dram_tensor("outT_dram", (D, ROWS), F32, kind="ExternalOutput").ap())
    build(nc, *args)
    r = _run(nc, [{f"{k}_dram": a for k, a in arrays.items()}], core_ids=[0])
    return r.results[0]["outT_dram"].T.reshape(2, 1024, D)
```
